# Optimizing a Trainium2 kernel written in Bass

```python
import numpy as np
import jax
import jax.numpy as jnp

def _softmax(x, axis=-1):
    return jax.nn.softmax(x, axis=axis)

def _gelu(x):
    return jax.nn.gelu(x, approximate=True)

def _silu(x):
    return jax.nn.silu(x)

def _sigmoid(x):
    return jax.nn.sigmoid(x)

def _layernorm(x, axis=-1, eps=1e-05):
    m = jnp.mean(x, axis=axis, keepdims=True)
    v = jnp.var(x, axis=axis, keepdims=True)
    return (x - m) / jnp.sqrt(v + eps)

def _scatter_add(tgt, idx, src, axis=0):
    return tgt.at[idx].add(src)

def _segment_sum(src, seg, n):
    return jax.ops.segment_sum(src, seg, n)
kernel_name = 'mk_adaln_d1_jaxref_r2_bbaf8e'

def setup_inputs(seed: int=0):
    np.random.seed(seed)
    _w = jnp.asarray

    def _L0_attn_setup():
        import jax, jax.numpy as jnp
        import numpy as np
        HIDDEN = 512
        STATE = 16
        BATCH = 4
        SEQ = 1024
        LN_EPS = 1e-05

        def _selective_scan(x_ssm, dt, A, Bm, Cm):
            Bsz, L, D = x_ssm.shape
            N = A.shape[1]

            def step(h, inp):
                xt, dtt, bt, ct = inp
                dA = jnp.exp(A[None] * dtt[..., None])
                dB = dtt[..., None] * bt[:, None, :]
                h = dA * h + dB * xt[..., None]
                y = jnp.sum(h * ct[:, None, :], axis=-1)
                return (h, y)
            h0 = jnp.zeros((Bsz, D, N), x_ssm.dtype)
            xs = (jnp.swapaxes(x_ssm, 0, 1), jnp.swapaxes(dt, 0, 1), jnp.swapaxes(Bm, 0, 1), jnp.swapaxes(Cm, 0, 1))
            _, ys = jax.lax.scan(step, h0, xs)
            return jnp.swapaxes(ys, 0, 1)
        key = jax.random.key(seed)
        ks = jax.random.split(key, 16)
        D, N = (HIDDEN, STATE)
        s = 0.02
        return {'x': jax.random.normal(ks[0], (BATCH, SEQ, D), dtype=jnp.float32), 'w_in': jax.random.normal(ks[1], (2 * D, D), dtype=jnp.float32) * s, 'b_in': jnp.zeros((2 * D,), jnp.float32), 'w_dt': jax.random.normal(ks[2], (D, D), dtype=jnp.float32) * s, 'b_dt': jnp.zeros((D,), jnp.float32), 'A_log': jax.random.normal(ks[3], (D, N), dtype=jnp.float32), 'w_B': jax.random.normal(ks[4], (N, D), dtype=jnp.float32) * s, 'b_B': jnp.zeros((N,), jnp.float32), 'w_C': jax.random.normal(ks[5], (N, D), dtype=jnp.float32) * s, 'b_C': jnp.zeros((N,), jnp.float32), 'D': jnp.ones((D,), jnp.float32), 'w_out': jax.random.normal(ks[6], (D, D), dtype=jnp.float32) * s, 'b_out': jnp.zeros((D,), jnp.float32), 'gamma': jnp.ones((D,), jnp.float32), 'beta': jnp.zeros((D,), jnp.float32)}
    _L0_attn_in = _L0_attn_setup()

    def _L0_ffn_setup():
        import jax, jax.numpy as jnp
        import numpy as np
        D_MODEL = 512
        M = 64
        INNER = 16
        key = jax.random.key(seed)
        ks = jax.random.split(key, 9)

        def init(k, shape, fan_in):
            bound = 1.0 / np.sqrt(fan_in)
            return jax.random.uniform(k, shape, jnp.float32, -bound, bound)
        x = jax.random.normal(ks[0], (16, 2048, D_MODEL), dtype=jnp.float32)
        Win = init(ks[1], (D_MODEL, M), D_MODEL)
        bin_ = init(ks[2], (M,), D_MODEL)
        W1 = init(ks[3], (M, INNER), 1)
        b1 = init(ks[4], (M, INNER), 1)
        W2 = init(ks[5], (M, INNER), INNER)
        b2 = init(ks[6], (M,), INNER)
        Wout = init(ks[7], (M, D_MODEL), M)
        bout = init(ks[8], (D_MODEL,), M)
        return {'x': x, 'Win': Win, 'bin_': bin_, 'W1': W1, 'b1': b1, 'W2': W2, 'b2': b2, 'Wout': Wout, 'bout': bout}
    _L0_ffn_in = _L0_ffn_setup()
    _L0_c = _w((lambda *s: np.random.randn(*s).astype(np.float32) * 0.05)(4, 512))
    _L0_wmod = _w((lambda *s: np.random.randn(*s).astype(np.float32) * 0.05)(512, 6 * 512) * 512 ** (-0.5))
    _d = {'L0_attn_x': _L0_attn_in['x'], 'L0_attn_w_in': _L0_attn_in['w_in'], 'L0_attn_b_in': _L0_attn_in['b_in'], 'L0_attn_w_dt': _L0_attn_in['w_dt'], 'L0_attn_b_dt': _L0_attn_in['b_dt'], 'L0_attn_A_log': _L0_attn_in['A_log'], 'L0_attn_w_B': _L0_attn_in['w_B'], 'L0_attn_b_B': _L0_attn_in['b_B'], 'L0_attn_w_C': _L0_attn_in['w_C'], 'L0_attn_b_C': _L0_attn_in['b_C'], 'L0_attn_D': _L0_attn_in['D'], 'L0_attn_w_out': _L0_attn_in['w_out'], 'L0_attn_b_out': _L0_attn_in['b_out'], 'L0_attn_gamma': _L0_attn_in['gamma'], 'L0_attn_beta': _L0_attn_in['beta'], 'L0_ffn_Win': _L0_ffn_in['Win'], 'L0_ffn_bin_': _L0_ffn_in['bin_'], 'L0_ffn_W1': _L0_ffn_in['W1'], 'L0_ffn_b1': _L0_ffn_in['b1'], 'L0_ffn_W2': _L0_ffn_in['W2'], 'L0_ffn_b2': _L0_ffn_in['b2'], 'L0_ffn_Wout': _L0_ffn_in['Wout'], 'L0_ffn_bout': _L0_ffn_in['bout'], 'L0_c': _L0_c, 'L0_wmod': _L0_wmod}
    _x0 = _d['L0_attn_x']
    _d['L0_attn_x'] = jax.random.normal(jax.random.fold_in(jax.random.key(seed), 1), (4, 4096, 512), dtype=_x0.dtype)
    del _x0
    return _d

def reference(L0_attn_x, L0_attn_w_in, L0_attn_b_in, L0_attn_w_dt, L0_attn_b_dt, L0_attn_A_log, L0_attn_w_B, L0_attn_b_B, L0_attn_w_C, L0_attn_b_C, L0_attn_D, L0_attn_w_out, L0_attn_b_out, L0_attn_gamma, L0_attn_beta, L0_ffn_Win, L0_ffn_bin_, L0_ffn_W1, L0_ffn_b1, L0_ffn_W2, L0_ffn_b2, L0_ffn_Wout, L0_ffn_bout, L0_c, L0_wmod):

    def _L0_attn_ref(x, w_in, b_in, w_dt, b_dt, A_log, w_B, b_B, w_C, b_C, D, w_out, b_out, gamma, beta):
        import jax, jax.numpy as jnp
        import numpy as np
        HIDDEN = 512
        STATE = 16
        BATCH = 4
        SEQ = 1024
        LN_EPS = 1e-05

        def _selective_scan(x_ssm, dt, A, Bm, Cm):
            Bsz, L, D = x_ssm.shape
            N = A.shape[1]

            def step(h, inp):
                xt, dtt, bt, ct = inp
                dA = jnp.exp(A[None] * dtt[..., None])
                dB = dtt[..., None] * bt[:, None, :]
                h = dA * h + dB * xt[..., None]
                y = jnp.sum(h * ct[:, None, :], axis=-1)
                return (h, y)
            h0 = jnp.zeros((Bsz, D, N), x_ssm.dtype)
            xs = (jnp.swapaxes(x_ssm, 0, 1), jnp.swapaxes(dt, 0, 1), jnp.swapaxes(Bm, 0, 1), jnp.swapaxes(Cm, 0, 1))
            _, ys = jax.lax.scan(step, h0, xs)
            return jnp.swapaxes(ys, 0, 1)
        residual = x
        xz = x @ w_in.T + b_in
        x_ssm, z = jnp.split(xz, 2, axis=-1)
        z = jax.nn.silu(z)
        dt = jax.nn.softplus(x_ssm @ w_dt.T + b_dt)
        Bm = x_ssm @ w_B.T + b_B
        Cm = x_ssm @ w_C.T + b_C
        A = -jnp.exp(A_log)
        y = _selective_scan(x_ssm, dt, A, Bm, Cm)
        y = y + D[None, None, :] * x_ssm
        y = y * z
        y = y @ w_out.T + b_out
        pre = y + residual
        mu = jnp.mean(pre, axis=-1, keepdims=True)
        var = jnp.mean(jnp.square(pre - mu), axis=-1, keepdims=True)
        return (pre - mu) * jax.lax.rsqrt(var + LN_EPS) * gamma + beta

    def _L0_ffn_ref(x, Win, bin_, W1, b1, W2, b2, Wout, bout):
        import jax, jax.numpy as jnp
        import numpy as np
        D_MODEL = 512
        M = 64
        INNER = 16
        s = jnp.einsum('btd,dm->btm', x, Win) + bin_
        h = jax.nn.relu(s[..., None] * W1 + b1)
        g = jnp.einsum('btmh,mh->btm', h, W2) + b2
        out = jnp.einsum('btm,md->btd', g, Wout) + bout
        return out
    x = L0_attn_x
    mod = (_silu(L0_c) @ L0_wmod).reshape(L0_c.shape[0], 6, 1, -1)
    sa, ca, ga, sb, cb, gb = (mod[:, 0], mod[:, 1], mod[:, 2], mod[:, 3], mod[:, 4], mod[:, 5])
    ga = (2 * (ga >= 0) - 1) * jnp.maximum(jnp.abs(ga), 0.25)
    gb = (2 * (gb >= 0) - 1) * jnp.maximum(jnp.abs(gb), 0.25)
    h = _layernorm(x, axis=-1) * (1 + ca) + sa
    x = x + ga * _L0_attn_ref(h, L0_attn_w_in, L0_attn_b_in, L0_attn_w_dt, L0_attn_b_dt, L0_attn_A_log, L0_attn_w_B, L0_attn_b_B, L0_attn_w_C, L0_attn_b_C, L0_attn_D, L0_attn_w_out, L0_attn_b_out, L0_attn_gamma, L0_attn_beta)
    h = _layernorm(x, axis=-1) * (1 + cb) + sb
    x = x + gb * _L0_ffn_ref(h, L0_ffn_Win, L0_ffn_bin_, L0_ffn_W1, L0_ffn_b1, L0_ffn_W2, L0_ffn_b2, L0_ffn_Wout, L0_ffn_bout)
    return x

_drawn_inputs = setup_inputs


def setup_inputs(seed=0):
    import zlib

    import numpy as np

    out = dict(_drawn_inputs(seed))
    spreads = {'L0_attn_b_in': (0.0, 0.8),
     'L0_attn_b_dt': (0.0, 2.0),
     'L0_attn_b_B': (0.0, 0.8),
     'L0_attn_b_C': (0.0, 2.0),
     'L0_attn_D': (1.0, 0.6),
     'L0_attn_b_out': (0.0, 2.0),
     'L0_attn_gamma': (1.0, 0.2),
     'L0_attn_beta': (0.0, 0.342)}
    factors = {'L0_attn_w_in': 4.219,
     'L0_attn_w_dt': 8.0,
     'L0_attn_A_log': 8.0,
     'L0_attn_w_B': 8.0,
     'L0_attn_w_C': 8.0,
     'L0_attn_w_out': 4.066,
     'L0_ffn_Win': 3.533,
     'L0_ffn_bin_': 8.0,
     'L0_ffn_W1': 3.457,
     'L0_ffn_bout': 3.324}
    for name, (base, spread) in spreads.items():
        noise = np.random.default_rng([zlib.crc32(name.encode()), seed]).standard_normal(out[name].shape)
        drawn = base * np.exp(spread * noise) if base else spread * noise
        out[name] = jnp.asarray(drawn.astype(out[name].dtype))
    for name, factor in factors.items():
        out[name] = (out[name] * factor).astype(out[name].dtype)
    return out
```

```python
def build_program(nc, ap, B, L, D, N, M, INNER):
    import concourse.bass as bass
    from concourse import mybir
    from contextlib import ExitStack

    f32 = mybir.dt.float32
    f32r = mybir.dt.float32r
    ALU = mybir.AluOpType
    ACT = mybir.ActivationFunctionType

    T = 128
    P = 128
    KD = D // P
    NB = L // T
    U = 64
    SU = T // U
    UNITS = KD * SU
    G = T // 32
    HN = N // 2
    J = INNER // 2
    EPS = 1e-5

    ctx = ExitStack()
    with ctx:
        def sb(name, shape, dt=f32):
            return ctx.enter_context(nc.sbuf_tensor(name, shape, dt))

        def pb(name, shape):
            return ctx.enter_context(nc.psum_tensor(name, shape, f32))

        def sem(name):
            return ctx.enter_context(nc.semaphore(name))

        w_in = sb("w_in_t", [P, KD, 2 * D])
        w_dt = sb("w_dt_t", [P, KD, D])
        w_out = sb("w_out_t", [P, KD, D])
        w_cb = sb("w_cb_t", [P, KD, 2 * N])
        win2 = sb("win2", [P, KD, 2 * M])
        ident = sb("ident", [P, P])
        mask = sb("mask", [P, 32])
        sel_c = sb("sel_c", [2 * 32, N, P], f32r)
        rows = sb("rows", [64 + 2 * N, D])
        ones = sb("ones", [64, P])
        sel_b_t = sb("sel_b", [64 + 2 * N, N])
        b_out, bout_g = rows[0:1, :], rows[32:33, :]
        b_rep = rows[64:64 + 2 * N, :].rearrange("p (g q t) -> p g q t", g=G, q=4)
        sel_b = sel_b_t[64:64 + 2 * N, :]
        b_in = sb("b_in_col", [P, 2 * KD])
        b_dt = sb("b_dt_col", [P, KD])
        d_skip = sb("d_skip_col", [P, KD])
        b_cb = sb("b_cb_col", [2 * N, 1])
        neg_a = sb("neg_a", [P, KD, N])
        w1 = sb("w1", [P, J])
        b1 = sb("b1", [P, J])
        w2 = sb("w2", [P, J])
        b2 = sb("b2", [P, 1])
        bin2 = sb("bin2", [P, 1])
        c_t = sb("c_t", [P, KD, B])
        c_tmp = sb("c_tmp", [P, KD, B])
        mod_all = sb("mod_all", [P, 4 * KD, B])
        mod = sb("mod", [P, 4 * KD])
        gain = sb("gain", [P, D])
        shift = sb("shift", [P, D])
        wout_g = sb("wout_g", [P, D])

        x_in = sb("x_in", [P, 2, D])
        x_res = sb("x_res", [P, 2, D])
        xn = sb("xn", [P, D])
        h_t = sb("h_t", [P, 2, KD, T])
        xs_t = sb("xs_t", [P, 2, KD, T])
        sz_t = sb("sz_t", [P, 2, KD, T])
        ez = ev = sb("ez", [P, KD, T])
        v_t = u_t = sb("v_t", [P, KD, T])
        dt_t = sb("dt_t", [P, 2, KD, T])
        u_hi = sb("u_hi", [P, D], f32r)
        u_lo = sb("u_lo", [P, D], f32r)
        u_st = sb("u_st", [P, 2, G, D], f32r)
        cb_t = sb("cb_t", [2 * N, T])
        c_st = sb("c_st", [2 * 32, T], f32r)
        b_st = sb("b_st", [P, G, N], f32r)
        b_dg = sb("b_dg", [P, 2, G, N, 32], f32r)
        c_bc = sb("c_bc", [P, 2, N, T])
        decay = sb("decay", [P, KD, SU, N, U])
        dec0 = sb("dec0", [P, SU, N])
        carry = sb("carry", [P, N])
        hs = sb("hs", [P, 4, N, U])
        state = sb("state", [P, KD, N])
        pr = sb("pr", [P, 2, N, T])
        yx = sb("yx", [P, T])
        xn2 = xn
        h2_t = sb("h2_t", [P, KD, T])
        rel = sb("rel", [P, J, T])
        t1 = rel[:, 0:D // T, :].rearrange("p a b -> p (a b)")
        gm = sb("gm", [P, T])
        st = [sb(f"st{n}", [P, 6]) for n in range(3)]
        mv = [sb(f"mv{n}", [P, 2]) for n in range(3)]
        lv = [sb(f"lv{n}", [P, 1]) for n in range(3)]
        rstd = [sb(f"rstd{n}", [P, 1]) for n in range(3)]
        eps = sb("eps", [P, 1])
        idle = sb("idle", [P, 1])

        work = decay[:, :, :, :, :].rearrange("p a b c d -> p (a b c d)")
        wm4 = work[:, 0:KD * 4 * D].rearrange("p (k n) -> p k n", k=KD)
        wmg = work[:, 0:KD * 2 * D].rearrange("p (k n) -> p k n", k=KD)
        row = lambda n: work[:, (2 * KD + n) * D:(2 * KD + n + 1) * D]
        gamma_b, beta_b, wout_b, bout_b, sign, gate_a, gate_b = (row(n) for n in range(7))
        c_rep = row(7).rearrange("p (k n) -> p k n", k=KD)

        b_ps = pb("b_ps", [P, 2, N * U])
        dn = [pb(f"dense{n}", [P, 512]) for n in range(2)]
        y_ps = [pb(f"y_ps{n}", [P, 512]) for n in range(2)]

        names = """w_loaded b2_loaded wm_loaded wmg_loaded rows_loaded x_loaded_even x_loaded_odd ust_loaded stored_even stored_odd
        const_zeroed const_masks sel_copied neg_done scal_done c_exp c_one c_rcp silu_c mods_ps mods_done
        c_rep_done gates_ps sign_done gate_done gates_done batch_ready
        st0_done mv0_done lv0_done rstd0_done xn_done xt_ps h_done xs_ps xs_done v_ps v_done ab_done ev_done
        lnv_done dt_done u_done u_ps uhi_done ulo_done z_ps z_done ez_done ez1_done ezr_done sz_done
        cb_ps cb_done chi_done clo_done brep_done bst_ps bhi_done blo_done bdg_done cbc_ps cbc_done xres_done
        dec_done dec0_done dec_zeroed carry_done b_ps_done b_fixed scan_done state_saved prod_done y_ps_done
        yx_done yz_done
        pre_ps st1_done mv1_done lv1_done rstd1_done t1_done tg_done x1_done st2_done mv2_done lv2_done
        rstd2_done xn2_done x2t_ps h2_done s_ps rel_done gm_done out_ps out_done""".split()
        S = {n: sem(n) for n in names}
        x_loaded = [S["x_loaded_even"], S["x_loaded_odd"]]
        stored = [S["stored_even"], S["stored_odd"]]
        Q = 16

        def x_count(k, p):
            return k * (Q // 2) + (Q - p * (Q // 2))

        N_WEIGHTS = 4 + 5 * 2 + 6
        N_UST = 4 * G

        blk = ctx.enter_context(nc.Block(no_gpsimd_drain=True))

        def batches(eng, start, part):
            with eng.Fori(0, B) as batch:
                start(batch)
                k = batch * NB
                part(k, None, None, 1)
                part(k + 1, k, None, 0)
                with eng.Fori(0, (NB - 2) // 2) as pair:
                    for m in (1, 2):
                        s = k + pair * 2 + m
                        part(s + 1, s, s - 1, m % 2)
                part(None, k + (NB - 1), k + (NB - 2), 1)
                part(None, None, k + (NB - 1), 0)

        @blk.sync
        def _(sp):
            def load(dst, src):
                sp.dma_start(dst, src).then_inc(S["w_loaded"], Q)

            load(w_in[:, :, :], ap["w_in_t"].rearrange("(k p) n -> p k n", p=P))
            load(w_dt[:, :, :], ap["w_dt_t"].rearrange("(k p) n -> p k n", p=P))
            load(w_out[:, :, :], ap["w_out_t"].rearrange("(k p) n -> p k n", p=P))
            load(w_cb[:, :, :], ap["w_cb_t"].rearrange("(k p) n -> p k n", p=P))
            for h in range(2):
                load(win2[:, :, h * M:(h + 1) * M], ap["Win"].rearrange("(k p) n -> p k n", p=P))
                load(bin2[h * M:(h + 1) * M, :], ap["bin"].rearrange("(p a) -> p a", a=1))
                for dst, src in ((w1, "W1"), (b1, "b1"), (w2, "W2")):
                    load(dst[h * M:(h + 1) * M, :], ap[src][:, h * J:(h + 1) * J])
            load(b_out, ap["b_out"].rearrange("(a n) -> a n", a=1))
            load(b_in[:, :], ap["b_in_c"])
            load(b_dt[:, :], ap["b_dt_c"])
            load(d_skip[:, :], ap["D_c"])
            load(b_cb[:, :], ap["b_cb"].rearrange("(p a) -> p a", a=1))
            load(neg_a[:, :, :], ap["A_log_c"])
            sp.dma_start(c_t[:, :, :], ap["c_t"]).then_inc(S["c_exp"], Q)
            sp.wait_ge(S["const_zeroed"], 6)
            sp.dma_start(b2[0:M, :], ap["b2"].rearrange("(p a) -> p a", a=1)).then_inc(S["b2_loaded"], Q)
            sp.wait_ge(S["sel_copied"], 1)
            for n, v in enumerate((0, 1, 3, 4)):
                sp.dma_start(wm4[:, :, n * D:(n + 1) * D],
                             ap["wmod"][:, v * D:(v + 1) * D].rearrange("(k p) n -> p k n", p=P)
                             ).then_inc(S["wm_loaded"], Q)
            sp.wait_ge(S["mods_ps"], 1)

            def load_x(k, p):
                sp.dma_start(x_in[:, p, :], ap["x"][bass.ds(k * T, T), :]).then_inc(x_loaded[p], Q)

            def start(batch):
                sp.wait_ge(S["out_done"], batch * NB)
                for n, v in enumerate((2, 5)):
                    sp.dma_start(wmg[:, :, n * D:(n + 1) * D],
                                 ap["wmod"][:, v * D:(v + 1) * D].rearrange("(k p) n -> p k n", p=P)
                                 ).then_inc(S["wmg_loaded"], Q)
                for dst, src in ((gamma_b, "gamma"), (beta_b, "beta"), (bout_b, "bout")):
                    sp.dma_start(dst, ap[src].rearrange("(a n) -> a n", a=1).to_broadcast([P, D])
                                 ).then_inc(S["rows_loaded"], Q)
                for h in range(2):
                    sp.dma_start(wout_b[h * M:(h + 1) * M, :], ap["Wout"]).then_inc(S["rows_loaded"], Q)
                load_x(batch * NB, 0)
                load_x(batch * NB + 1, 1)

            def part(f, s, b, p, more=True):
                q = 1 - p
                if s is not None and more:
                    sp.wait_ge(S["xn_done"], s + 1)
                    sp.wait_ge(S["xres_done"], s + 1)
                    load_x(s + 2, p)
                if f is not None:
                    sp.wait_ge(S["uhi_done"], f + 1)
                    sp.wait_ge(S["ulo_done"], f + 1)
                    for quad, src in enumerate((u_hi, u_hi, u_lo, u_lo)):
                        for g in range(G):
                            sp.dma_start(u_st[32 * quad:32 * quad + 32, q, g, :].bitcast(f32),
                                         src[32 * g:32 * g + 32, :].bitcast(f32)).then_inc(S["ust_loaded"], Q)
                if b is not None:
                    sp.wait_ge(S["out_done"], b + 1)
                    sp.dma_start(ap["out"][bass.ds(b * T, T), :], x_res[:, q, :]).then_inc(stored[q], Q)

            with sp.Fori(0, B) as batch:
                start(batch)
                k = batch * NB
                part(k, None, None, 1)
                part(k + 1, k, None, 0)
                with sp.Fori(0, (NB - 4) // 2) as pair:
                    for m in (1, 2):
                        s = k + pair * 2 + m
                        part(s + 1, s, s - 1, m % 2)
                part(k + (NB - 2), k + (NB - 3), k + (NB - 4), 1)
                part(k + (NB - 1), k + (NB - 2), k + (NB - 3), 0, more=False)
                part(None, k + (NB - 1), k + (NB - 2), 1, more=False)
                part(None, None, k + (NB - 1), 0)
            for n in range(2):
                sp.wait_ge(stored[n], Q * B * NB // 2)

        @blk.gpsimd
        def _(gp):
            f_sel = work[0:64, 0:N * P].rearrange("p (n c) -> p n c", n=N)
            for t, v in ((ident, 0.0), (mask, 0.0), (sel_b_t, 0.0), (ones, 1.0), (b2, 0.0)):
                gp.memset(t[:, :], v).then_inc(S["const_zeroed"], 1)
            gp.memset(f_sel, 0.0).then_inc(S["const_zeroed"], 1)
            gp.wait_ge(S["const_zeroed"], 6)

            def select(view, base, pattern, n):
                gp.affine_select(out=view, in_=view, compare_op=ALU.not_equal, fill=1.0, base=base,
                                 pattern=pattern, channel_multiplier=1).then_inc(S["const_masks"], 1)
                gp.wait_ge(S["const_masks"], n)

            select(ident[:, :], 0, [[-1, P]], 1)
            for q in range(4):
                select(mask[:, :], -32 * q, [[-1, 32]], 2 + q)
            select(sel_b, -N, [[-1, N]], 6)
            for q in range(2):
                select(f_sel, -32 * q, [[-1, N], [0, P]], 7 + q)

            def start(batch):
                gp.wait_ge(S["batch_ready"], batch + 1)
                for n in range(2):
                    gp.wait_ge(stored[n], batch * (NB * Q // 2))

            def part(f, s, b, p):
                q = 1 - p
                for u in range(UNITS):
                    j, half = u // SU, u % SU
                    if s is not None:
                        gp.wait_ge(S["scan_done"], s * UNITS + (u + 1))
                        if u == 0:
                            gp.wait_ge(S["cbc_done"], s * 4 + 4)
                        if half == 0 and (b is not None or j >= 2):
                            gp.wait_ge(S["y_ps_done"], s * KD + (j - 1))
                        gp.tensor_tensor(pr[:, j % 2, :, half * U:(half + 1) * U], hs[:, u % 4, :, :],
                                         c_bc[:, p, :, half * U:(half + 1) * U], ALU.mult
                                         ).then_inc(S["prod_done"], 1)
                    if u == 3 and b is not None:
                        gp.wait_ge(S["t1_done"], b + 1)
                        gp.tensor_tensor(t1[:, :], t1[:, :], gain[:, :], ALU.mult).then_inc(S["tg_done"], 1)
                        gp.wait_ge(S["tg_done"], b + 1)
                        gp.tensor_tensor(x_res[:, q, :], x_res[:, q, :], t1[:, :], ALU.add
                                         ).then_inc(S["x1_done"], 1)
                    if u == 5 and s is not None:
                        gp.wait_ge(x_loaded[p], x_count(s, p))
                        if b is not None:
                            gp.wait_ge(stored[p], s * (Q // 2) - p * (Q // 2))
                        gp.tensor_tensor(x_res[:, p, :], x_in[:, p, :], shift[:, :], ALU.add
                                         ).then_inc(S["xres_done"], 1)
                    if u == 6 and f is not None:
                        gp.wait_ge(S["dt_done"], f + 1)
                        gp.wait_ge(S["u_ps"], f)
                        gp.tensor_tensor(u_t[:, :, :], dt_t[:, q, :, :], xs_t[:, q, :, :], ALU.mult
                                         ).then_inc(S["u_done"], 1)

            batches(gp, start, part)

        @blk.tensor
        def _(pe):
            mm = nc.tensor.matmul
            pe.wait_ge(S["w_loaded"], Q * N_WEIGHTS)
            pe.wait_ge(S["const_masks"], 8)
            pe.wait_ge(S["silu_c"], 1)
            pe.wait_ge(S["wm_loaded"], Q * 4)
            for m in range(4 * KD):
                for j in range(KD):
                    last = mm(dn[0][:, m * B:(m + 1) * B], wm4[:, j, m * P:(m + 1) * P], c_t[:, j, :],
                              start=(j == 0), stop=(j == KD - 1))
            last.then_inc(S["mods_ps"], 1)
            pe.wait_ge(S["mods_done"], 2)

            def start(batch):
                pe.wait_ge(S["c_rep_done"], batch + 1)
                pe.wait_ge(S["wmg_loaded"], batch * (2 * Q) + 2 * Q)
                pe.wait_ge(S["out_done"], batch * NB)
                for n in range(2):
                    for j in range(KD):
                        last = mm(dn[n][:, :], c_rep[:, j, :], wmg[:, j, n * D:(n + 1) * D],
                                  start=(j == 0), stop=(j == KD - 1))
                last.then_inc(S["gates_ps"], 1)
                pe.wait_ge(S["batch_ready"], batch + 1)

            def scan_input(s, p, u, first):
                j, half = u // SU, u % SU
                if u == 0:
                    pe.wait_ge(S["bdg_done"], s + 1)
                    pe.wait_ge(S["ust_loaded"], s * (Q * N_UST) + Q * N_UST)
                if u >= 2 or not first:
                    pe.wait_ge(S["scan_done"], s * UNITS + (u - 1))
                for g in range(2):
                    for h in range(2):
                        bank = b_ps[:, u % 2, h * 512:(h + 1) * 512].rearrange("p (n t) -> p n t", t=U)
                        last = mm(bank[:, :, g * 32:(g + 1) * 32],
                                  u_st[:, p, 2 * half + g, j * P:(j + 1) * P],
                                  b_dg[:, p, 2 * half + g, h * HN:(h + 1) * HN, :], start=True, stop=True)
                last.then_inc(S["b_ps_done"], 1)

            def sum_states(s, j, first):
                pe.wait_ge(S["prod_done"], s * UNITS + SU * (j + 1))
                if j >= 2 or not first:
                    pe.wait_ge(S["yx_done"], s * KD + (j - 1))
                for n in range(N):
                    last = mm(y_ps[j % 2][:, 0:T], ident[:, :], pr[:, j % 2, n, :], start=(n == 0),
                              stop=(n == N - 1))
                last.then_inc(S["y_ps_done"], 1)

            def transpose4(dst, src, ready):
                for j in range(KD):
                    last = nc.tensor.transpose(dst[:, j * P:(j + 1) * P], src[:, j * P:(j + 1) * P], ident[:, :])
                last.then_inc(ready, 1)

            def project(dst, w, col, src, ready):
                for m in range(KD):
                    for j in range(KD):
                        last = mm(dst[:, m * T:(m + 1) * T], w[:, j, col + m * P:col + (m + 1) * P], src[:, j, :],
                                  start=(j == 0), stop=(j == KD - 1))
                last.then_inc(ready, 1)

            def part(f, s, b, p):
                q = 1 - p
                first = b is None
                if s is not None:
                    scan_input(s, p, 0, first)
                for u in range(UNITS):
                    if s is not None and u + 1 < UNITS:
                        scan_input(s, p, u + 1, first)
                    if u == 0 and b is not None:
                        sum_states(b, KD - 1, False)
                    if u in (3, 5, 7) and s is not None:
                        sum_states(s, (u - 3) // 2, first)
                    if u == 1 and f is not None:
                        if s is not None:
                            pe.wait_ge(S["cbc_done"], s * 4 + 4)
                        if b is not None:
                            pe.wait_ge(S["out_done"], b)
                        pe.wait_ge(S["xn_done"], f + 1)
                        transpose4(dn[1], xn, S["xt_ps"])
                    if u == 2 and b is not None:
                        if s is not None:
                            pe.wait_ge(S["z_done"], s + 1)
                        else:
                            pe.wait_ge(S["h2_done"], b * KD)
                        pe.wait_ge(S["yz_done"], b * KD + KD)
                        mm(dn[0][:, :], ones[0:1, :], b_out, start=True, stop=False)
                        for j in range(KD):
                            mm(dn[0][:, j * P:(j + 1) * P], h_t[:, q, j, :], ident[:, :], start=False, stop=False)
                        for j in range(KD):
                            last = mm(dn[0][:, :], sz_t[:, q, j, :], w_out[:, j, :], start=False,
                                      stop=(j == KD - 1))
                        last.then_inc(S["pre_ps"], 1)
                    if u == 3 and f is not None:
                        if b is not None:
                            pe.wait_ge(S["t1_done"], b + 1)
                        elif s is not None:
                            pe.wait_ge(S["z_done"], s + 1)
                        pe.wait_ge(S["h_done"], f * KD + KD)
                        project(dn[0], w_in, 0, h_t[:, q, :, :], S["xs_ps"])
                    if u == 4 and f is not None:
                        pe.wait_ge(S["xs_done"], f + 1)
                        project(dn[1], w_dt, 0, xs_t[:, q, :, :], S["v_ps"])
                    if u == 5 and f is not None:
                        pe.wait_ge(S["v_done"], f + 1)
                        for j in range(KD):
                            last = mm(dn[1][0:2 * N, 0:T], w_cb[:, j, :], xs_t[:, q, j, :], start=(j == 0),
                                      stop=(j == KD - 1))
                        last.then_inc(S["cb_ps"], 1)
                    if u == 5 and b is not None:
                        if f is not None:
                            pe.wait_ge(S["xs_done"], f + 1)
                        pe.wait_ge(S["t1_done"], b + 1)
                        pe.wait_ge(S["xn2_done"], b + 1)
                        transpose4(dn[0], xn2, S["x2t_ps"])
                    if u == 6 and f is not None:
                        pe.wait_ge(S["brep_done"], f + 1)
                        for g in range(G):
                            last = mm(dn[1][:, T + g * N:T + (g + 1) * N],
                                      b_rep[:, g, :, :].rearrange("p a b -> p (a b)"), sel_b,
                                      start=True, stop=True)
                        last.then_inc(S["bst_ps"], 1)
                        pe.wait_ge(S["clo_done"], f + 1)
                        pe.wait_ge(S["blo_done"], f * 2 + 2)
                        for c in range(4):
                            if c == 1:
                                if b is not None:
                                    pe.wait_ge(S["h2_done"], b * KD + KD)
                                else:
                                    pe.wait_ge(S["xs_done"], f + 1)
                            if c >= 2:
                                pe.wait_ge(S["cbc_done"], f * 4 + (c - 1))
                            for n in range(4):
                                last = mm(dn[(c + 1) % 2][:, n * T:(n + 1) * T], sel_c[:, 4 * c + n, :], c_st[:, :],
                                          start=True, stop=True)
                            last.then_inc(S["cbc_ps"], 1)
                    if u == 6 and b is not None:
                        if f is not None:
                            pe.wait_ge(S["cbc_done"], f * 4 + 3)
                        else:
                            pe.wait_ge(S["out_done"], b)
                        pe.wait_ge(S["h2_done"], b * KD + KD)
                        for j in range(KD):
                            last = mm(dn[1][:, 0:T], win2[:, j, :], h2_t[:, j, :], start=(j == 0),
                                      stop=(j == KD - 1))
                        last.then_inc(S["s_ps"], 1)
                    if u == 7 and f is not None:
                        pe.wait_ge(S["cbc_done"], f * 4 + 4)
                        pe.wait_ge(S["u_done"], f + 1)
                        transpose4(dn[0], u_t[:, :, :].rearrange("p a b -> p (a b)"), S["u_ps"])
                        pe.wait_ge(S["ulo_done"], f + 1)
                        project(dn[0], w_in, D, h_t[:, q, :, :], S["z_ps"])
                    if u == 7 and b is not None:
                        pe.wait_ge(S["gm_done"], b * J + J)
                        mm(dn[1][:, :], gm[:, :], wout_g[:, :], start=True, stop=False)
                        mm(dn[1][:, :], ones[32:33, :], bout_g, start=False, stop=True).then_inc(S["out_ps"], 1)

            batches(pe, start, part)

        @blk.scalar
        def _(act):
            A = nc.scalar.activation
            nc.scalar.preload_act_table_set("natural_log_exp_and_others")
            act.wait_ge(S["w_loaded"], Q * N_WEIGHTS)
            A(neg_a[:, :, :], neg_a[:, :, :], ACT.Exp).then_inc(S["neg_done"], 1)
            act.wait_ge(S["c_exp"], Q)
            A(c_tmp[:, :, :], c_t[:, :, :], ACT.Exp, scale=-1.0).then_inc(S["c_exp"], 1)

            def start(batch):
                act.wait_ge(S["scal_done"], 1)
                act.wait_ge(S["batch_ready"], batch + 1)

            def decays(k, p, j, h, first):
                if h == 0:
                    if j == 0:
                        act.wait_ge(S["dt_done"], k + 1)
                    if not first:
                        act.wait_ge(S["scan_done"], k * UNITS + (SU * (j + 1) - UNITS))
                for n in range(h * HN, (h + 1) * HN):
                    last = A(decay[:, j, :, n, :], dt_t[:, p, j, :].rearrange("p (s t) -> p s t", s=SU), ACT.Exp,
                             scale=neg_a[:, j, n:n + 1])
                last.then_inc(S["dec_done"], 1)

            def inv_std(n, k):
                act.wait_ge(S[f"mv{n}_done"], k + 1)
                A(lv[n][:, :], mv[n][:, 1:2], ACT.Ln, bias=eps[:, :]).then_inc(S[f"lv{n}_done"], 1)
                act.wait_ge(S[f"lv{n}_done"], k + 1)
                A(rstd[n][:, :], lv[n][:, :], ACT.Exp, scale=-0.5).then_inc(S[f"rstd{n}_done"], 1)

            def modulate(dst, psum, done, scale, shift_):
                for j in range(KD):
                    A(dst[:, j, :], psum[:, j * T:(j + 1) * T], ACT.Identity, scale=mod[:, scale + j:scale + j + 1],
                      bias=mod[:, shift_ + j:shift_ + j + 1]).then_inc(done, 1)

            def part(f, s, b, p):
                q = 1 - p
                first = b is None
                for u in range(UNITS):
                    if u == 0 and f is not None:
                        inv_std(0, f)
                    if u < UNITS - SU and s is not None:
                        decays(s, p, u // SU + 1, u % SU, first)
                    if u >= UNITS - SU and f is not None:
                        decays(f, q, 0, u % SU, s is None)
                    if u == 2 and f is not None:
                        act.wait_ge(S["xt_ps"], f + 1)
                        if b is not None:
                            act.wait_ge(S["pre_ps"], b + 1)
                        modulate(h_t[:, q, :, :], dn[1], S["h_done"], KD, 0)
                    if u == 2 and b is not None:
                        inv_std(1, b)
                    if u == 4 and b is not None:
                        inv_std(2, b)
                    if u == 5 and f is not None:
                        act.wait_ge(S["v_done"], f + 1)
                        act.wait_ge(S["sz_done"], f)
                        A(ev[:, :, :], v_t[:, :, :], ACT.Abs).then_inc(S["ab_done"], 1)
                        act.wait_ge(S["ab_done"], f + 1)
                        A(ev[:, :, :], ev[:, :, :], ACT.Exp, scale=-1.0).then_inc(S["ev_done"], 1)
                        act.wait_ge(S["ev_done"], f + 1)
                        A(ev[:, :, :], ev[:, :, :], ACT.Ln, bias=1.0).then_inc(S["lnv_done"], 1)
                        act.wait_ge(S["cb_ps"], f + 1)
                        act.wait_ge(S["brep_done"], f)
                        A(cb_t[:, :], dn[1][0:2 * N, 0:T], ACT.Identity, bias=b_cb[:, :]).then_inc(S["cb_done"], 1)
                    if u == 5 and b is not None:
                        act.wait_ge(S["x2t_ps"], b + 1)
                        act.wait_ge(S["s_ps"], b)
                        modulate(h2_t, dn[0], S["h2_done"], 3 * KD, 2 * KD)
                    if u == 6 and f is not None:
                        if b is not None:
                            act.wait_ge(S["prod_done"], b * UNITS + UNITS)
                        for c in range(4):
                            act.wait_ge(S["cbc_ps"], f * 4 + (c + 1))
                            A(c_bc[:, q, 4 * c:4 * c + 4, :], dn[(c + 1) % 2][:, :].rearrange("p (n t) -> p n t", n=4),
                              ACT.Copy).then_inc(S["cbc_done"], 1)
                    if u == 6 and b is not None:
                        act.wait_ge(S["s_ps"], b + 1)
                        act.wait_ge(S["gm_done"], b * J)
                        for j in range(J):
                            A(rel[:, j, :], dn[1][:, 0:T], ACT.Relu, scale=w1[:, j:j + 1], bias=b1[:, j:j + 1]
                              ).then_inc(S["rel_done"], 1)
                    if u == 7 and f is not None:
                        act.wait_ge(S["u_ps"], f + 1)
                        act.wait_ge(S["ust_loaded"], f * (Q * N_UST))
                        A(u_hi[:, :], dn[0][:, :], ACT.Copy).then_inc(S["uhi_done"], 1)
                        act.wait_ge(S["z_done"], f + 1)
                        act.wait_ge(S["dt_done"], f + 1)
                        A(ez[:, :, :], sz_t[:, q, :, :], ACT.Exp, scale=-1.0).then_inc(S["ez_done"], 1)

            batches(act, start, part)

        @blk.vector
        def _(dve):
            V = nc.vector

            def inc(ins, name, v):
                ins.then_inc(S[name], 1)
                dve.wait_ge(S[name], v)

            dve.wait_ge(S["const_masks"], 8)
            V.tensor_copy(sel_c[:, :, :], work[0:64, 0:N * P].rearrange("p (n c) -> p n c", n=N)
                          ).then_inc(S["sel_copied"], 1)
            V.memset(eps[:, :], EPS)
            dve.wait_ge(S["c_exp"], Q + 1)
            V.tensor_scalar(c_tmp[:, :, :], c_tmp[:, :, :], 1.0, None, ALU.add).then_inc(S["c_one"], 1)
            dve.wait_ge(S["c_one"], 1)
            V.reciprocal(c_tmp[:, :, :], c_tmp[:, :, :]).then_inc(S["c_rcp"], 1)
            dve.wait_ge(S["c_rcp"], 1)
            V.tensor_tensor(c_t[:, :, :], c_t[:, :, :], c_tmp[:, :, :], ALU.mult).then_inc(S["silu_c"], 1)
            dve.wait_ge(S["neg_done"], 1)
            V.tensor_scalar(neg_a[:, :, :], neg_a[:, :, :], -1.0, None, ALU.mult)
            dve.wait_ge(S["w_loaded"], Q * N_WEIGHTS)
            dve.wait_ge(S["b2_loaded"], Q)
            V.scalar_tensor_tensor(b1[:, :], w1[:, :], bin2[:, :], b1[:, :], ALU.mult, ALU.add
                                   ).then_inc(S["scal_done"], 1)
            dve.wait_ge(S["mods_ps"], 1)
            for n, plus in enumerate((0.0, 1.0, 0.0, 1.0)):
                last = V.tensor_scalar(mod_all[:, n * KD:(n + 1) * KD, :],
                                       dn[0][:, n * KD * B:(n + 1) * KD * B].rearrange("p (m b) -> p m b", b=B),
                                       plus, None, ALU.add)
            last.then_inc(S["mods_done"], 2)

            def start(batch):
                dve.wait_ge(S["mods_done"], 2)
                dve.wait_ge(S["silu_c"], 1)
                V.tensor_copy(c_rep[:, :, :], c_t[:, :, bass.ds(batch, 1)].to_broadcast([P, KD, P])
                              ).then_inc(S["c_rep_done"], 1)
                V.tensor_copy(mod[:, :], mod_all[:, :, bass.ds(batch, 1)].rearrange("p m b -> p (m b)"))
                V.memset(state[:, :, :], 0.0)
                dve.wait_ge(S["rows_loaded"], batch * (5 * Q) + 5 * Q)
                dve.wait_ge(S["gates_ps"], batch + 1)
                for n, gate in enumerate((gate_a, gate_b)):
                    V.tensor_scalar(sign, dn[n][:, :], 0.0, 2.0, ALU.is_ge, ALU.mult).then_inc(S["sign_done"], 1)
                    dve.wait_ge(S["sign_done"], batch * 6 + (3 * n + 1))
                    V.tensor_scalar(sign, sign, -1.0, None, ALU.add).then_inc(S["sign_done"], 1)
                    dve.wait_ge(S["sign_done"], batch * 6 + (3 * n + 2))
                    V.tensor_tensor(gate, sign, dn[n][:, :], ALU.mult).then_inc(S["sign_done"], 1)
                    dve.wait_ge(S["sign_done"], batch * 6 + (3 * n + 3))
                    V.scalar_tensor_tensor(gate, gate, 0.25, sign, ALU.max, ALU.mult).then_inc(S["gate_done"], 1)
                    dve.wait_ge(S["gate_done"], batch * 2 + (n + 1))
                V.tensor_tensor(gain[:, :], gate_a, gamma_b, ALU.mult)
                V.tensor_tensor(shift[:, :], gate_a, beta_b, ALU.mult)
                V.tensor_tensor(wout_g[:, :], gate_b, wout_b, ALU.mult)
                V.tensor_tensor(bout_g, gate_b[32:33, :], bout_b[32:33, :], ALU.mult
                                ).then_inc(S["batch_ready"], 1)
                dve.wait_ge(S["batch_ready"], batch + 1)

            def scan_unit(s, p, u, first):
                j, half = u // SU, u % SU
                if half == 0:
                    dve.wait_ge(S["dec_done"], s * (2 * KD) + (2 * j + 2))
                    V.tensor_copy(dec0[:, :, :], decay[:, j, :, :, 0]).then_inc(S["dec0_done"], 1)
                    dve.wait_ge(S["dec0_done"], s * KD + (j + 1))
                    V.memset(decay[:, j, :, :, 0], 0.0).then_inc(S["dec_zeroed"], 1)
                    if not first:
                        dve.wait_ge(S["state_saved"], s * KD + (j + 1 - KD))
                    before = state[:, j, :]
                else:
                    before = hs[:, (u - 1) % 4, :, U - 1]
                    dve.wait_ge(S["scan_done"], s * UNITS + u)
                V.tensor_tensor(carry[:, :], dec0[:, half, :], before, ALU.mult).then_inc(S["carry_done"], 1)
                dve.wait_ge(S["carry_done"], s * UNITS + (u + 1))
                dve.wait_ge(S["b_ps_done"], s * UNITS + (u + 1))
                inputs = b_ps[:, u % 2, :]
                heads = inputs.rearrange("p (n t) -> p n t", t=U)[:, :, 0]
                V.tensor_tensor(heads, heads, carry[:, :], ALU.add).then_inc(S["b_fixed"], 1)
                dve.wait_ge(S["b_fixed"], s * UNITS + (u + 1))
                dve.wait_ge(S["dec_zeroed"], s * KD + (j + 1))
                if u >= 4 or not first:
                    dve.wait_ge(S["prod_done"], s * UNITS + (u - 3))
                V.tensor_tensor_scan(hs[:, u % 4, :, :].rearrange("p n t -> p (n t)"),
                                     decay[:, j, half, :, :].rearrange("p n t -> p (n t)"), inputs, 0.0,
                                     ALU.mult, ALU.add).then_inc(S["scan_done"], 1)
                if half == SU - 1:
                    dve.wait_ge(S["scan_done"], s * UNITS + (u + 1))
                    V.tensor_copy(state[:, j, :], hs[:, u % 4, :, U - 1]).then_inc(S["state_saved"], 1)

            def gate_y(s, p, j):
                dve.wait_ge(S["yz_done"], s * KD + j)
                dve.wait_ge(S["y_ps_done"], s * KD + (j + 1))
                V.scalar_tensor_tensor(yx[:, :], xs_t[:, p, j, :], d_skip[:, j:j + 1], y_ps[j % 2][:, 0:T],
                                       ALU.mult, ALU.add).then_inc(S["yx_done"], 1)
                dve.wait_ge(S["yx_done"], s * KD + (j + 1))
                V.tensor_tensor(sz_t[:, p, j, :], sz_t[:, p, j, :], yx[:, :], ALU.mult).then_inc(S["yz_done"], 1)

            def moments(n, k, src):
                V.bn_stats(st[n][:, :], src).then_inc(S[f"st{n}_done"], 1)
                dve.wait_ge(S[f"st{n}_done"], k + 1)
                V.memset(idle[:, :], 0.0)
                V.bn_aggr(mv[n][:, :], st[n][:, :]).then_inc(S[f"mv{n}_done"], 1)

            def normalize(n, k, dst, src, done):
                dve.wait_ge(S[f"rstd{n}_done"], k + 1)
                V.tensor_scalar(dst, src, mv[n][:, 0:1], rstd[n][:, :], ALU.subtract, ALU.mult).then_inc(done, 1)

            def bias4(dst, psum, bias, done):
                V.tensor_tensor(dst, psum[:, :].rearrange("p (k t) -> p k t", k=KD),
                                bias.unsqueeze(2).to_broadcast([P, KD, T]), ALU.add).then_inc(done, 1)

            def part(f, s, b, p):
                q = 1 - p
                first = b is None
                for u in range(UNITS):
                    if u == 0 and f is not None:
                        dve.wait_ge(x_loaded[q], x_count(f, q))
                        dve.wait_ge(S["xn_done"], f)
                        moments(0, f, x_in[:, q, :])
                    if u == 0 and s is not None:
                        dve.wait_ge(S["ez_done"], s + 1)
                        V.tensor_scalar(ez[:, :, :], ez[:, :, :], 1.0, None, ALU.add).then_inc(S["ez1_done"], 1)
                        dve.wait_ge(S["ez1_done"], s + 1)
                        V.reciprocal(ez[:, :, :], ez[:, :, :]).then_inc(S["ezr_done"], 1)
                        dve.wait_ge(S["ezr_done"], s + 1)
                        V.tensor_tensor(sz_t[:, p, :, :], sz_t[:, p, :, :], ez[:, :, :], ALU.mult
                                        ).then_inc(S["sz_done"], 1)
                        dve.wait_ge(S["sz_done"], s + 1)
                    if u == 1 and b is not None:
                        gate_y(b, q, KD - 1)
                    if u == 1 and f is not None:
                        dve.wait_ge(S["xt_ps"], f)
                        if b is not None:
                            dve.wait_ge(S["x2t_ps"], b)
                        normalize(0, f, xn[:, :], x_in[:, q, :], S["xn_done"])
                    if u == 3 and b is not None:
                        dve.wait_ge(S["gm_done"], b * J)
                        normalize(1, b, t1[:, :], dn[0][:, :], S["t1_done"])
                    if u == 4 and f is not None:
                        dve.wait_ge(S["xs_ps"], f + 1)
                        bias4(xs_t[:, q, :, :], dn[0], b_in[:, 0:KD], S["xs_done"])
                    if u == 4 and s is not None:
                        gate_y(s, p, 0)
                    if u == 5 and b is not None:
                        if f is not None:
                            dve.wait_ge(S["xt_ps"], f + 1)
                        normalize(2, b, xn2[:, :], x_res[:, q, :], S["xn2_done"])
                    if u == 5 and f is not None:
                        dve.wait_ge(S["v_ps"], f + 1)
                        dve.wait_ge(S["u_ps"], f)
                        bias4(v_t[:, :, :], dn[1], b_dt[:, :], S["v_done"])
                    if u == 6 and s is not None:
                        gate_y(s, p, 1)
                    if u == 6 and f is not None:
                        dve.wait_ge(S["cb_done"], f + 1)
                        dve.wait_ge(S["cbc_ps"], f * 4)
                        V.tensor_copy(c_st[0:32, :], cb_t[:, :]).then_inc(S["chi_done"], 1)
                        dve.wait_ge(S["chi_done"], f + 1)
                        V.tensor_tensor(c_st[32:64, :], cb_t[:, :], c_st[0:32, :].bitcast(f32), ALU.subtract
                                        ).then_inc(S["clo_done"], 1)
                        dve.wait_ge(S["bst_ps"], f)
                        V.tensor_copy(b_rep,
                                      cb_t[:, :].rearrange("p (g o t) -> p g o t", g=G, o=1
                                                           ).to_broadcast([2 * N, G, 4, 32])
                                      ).then_inc(S["brep_done"], 1)
                    if s is not None:
                        scan_unit(s, p, u, first)
                    if u == 2 and b is not None:
                        dve.wait_ge(S["pre_ps"], b + 1)
                        moments(1, b, dn[0][:, :])
                    if u == 4 and b is not None:
                        dve.wait_ge(S["x1_done"], b + 1)
                        moments(2, b, x_res[:, q, :])
                    if u == 5 and f is not None:
                        dve.wait_ge(S["lnv_done"], f + 1)
                        V.scalar_tensor_tensor(dt_t[:, q, :, :].rearrange("p k t -> p (k t)"),
                                               v_t[:, :, :].rearrange("p k t -> p (k t)"), 0.0,
                                               ev[:, :, :].rearrange("p k t -> p (k t)"), ALU.max, ALU.add
                                               ).then_inc(S["dt_done"], 1)
                    if u == 6 and f is not None:
                        dve.wait_ge(S["bst_ps"], f + 1)
                        dve.wait_ge(S["bdg_done"], f)
                        src = dn[1][:, T:T + G * N].rearrange("p (g n) -> p g n", g=G)
                        V.tensor_copy(b_st[:, :, :], src).then_inc(S["bhi_done"], 1)
                        dve.wait_ge(S["bhi_done"], f + 1)
                        for quad in (1, 3):
                            rows = slice(32 * quad, 32 * quad + 32)
                            V.tensor_tensor(b_st[rows, :, :], src[rows], b_st[rows, :, :].bitcast(f32),
                                            ALU.subtract).then_inc(S["blo_done"], 1)
                        dve.wait_ge(S["blo_done"], f * 2 + 2)
                        for g in range(G):
                            last = V.tensor_tensor(
                                b_dg[:, q, g, :, :], mask[:, :].unsqueeze(1).to_broadcast([P, N, 32]),
                                b_st[:, g, :].bitcast(f32).unsqueeze(2).to_broadcast([P, N, 32]), ALU.mult)
                        last.then_inc(S["bdg_done"], 1)
                    if u == 7 and b is not None:
                        dve.wait_ge(S["rel_done"], b * J + J)
                        dve.wait_ge(S["out_ps"], b)
                        V.tensor_scalar(gm[:, :], rel[:, 0, :], w2[:, 0:1], b2[:, :], ALU.mult, ALU.add
                                        ).then_inc(S["gm_done"], 1)
                        for j in range(1, J):
                            dve.wait_ge(S["gm_done"], b * J + j)
                            V.scalar_tensor_tensor(gm[:, :], rel[:, j, :], w2[:, j:j + 1], gm[:, :], ALU.mult,
                                                   ALU.add).then_inc(S["gm_done"], 1)
                    if u == 7 and f is not None:
                        dve.wait_ge(S["uhi_done"], f + 1)
                        V.tensor_tensor(u_lo[:, :], dn[0][:, :], u_hi[:, :].bitcast(f32), ALU.subtract
                                        ).then_inc(S["ulo_done"], 1)
                        dve.wait_ge(S["z_ps"], f + 1)
                        bias4(sz_t[:, q, :, :], dn[0], b_in[:, KD:2 * KD], S["z_done"])
                    if u == 7 and b is not None:
                        dve.wait_ge(S["out_ps"], b + 1)
                        V.tensor_tensor(x_res[:, q, :], x_res[:, q, :], dn[1][:, :], ALU.add
                                        ).then_inc(S["out_done"], 1)
                    if u == 7 and s is not None:
                        gate_y(s, p, 2)

            batches(dve, start, part)


def kernel(L0_attn_x, L0_attn_w_in, L0_attn_b_in, L0_attn_w_dt, L0_attn_b_dt, L0_attn_A_log, L0_attn_w_B,
           L0_attn_b_B, L0_attn_w_C, L0_attn_b_C, L0_attn_D, L0_attn_w_out, L0_attn_b_out, L0_attn_gamma,
           L0_attn_beta, L0_ffn_Win, L0_ffn_bin_, L0_ffn_W1, L0_ffn_b1, L0_ffn_W2, L0_ffn_b2, L0_ffn_Wout,
           L0_ffn_bout, L0_c, L0_wmod):
    import numpy as np
    import concourse.bacc as bacc
    from concourse import mybir
    from concourse.bass_utils import run_bass_kernel_spmd

    B, L, D = L0_attn_x.shape
    N = L0_attn_A_log.shape[1]
    M, INNER = L0_ffn_W1.shape
    P = 128
    a = np.asarray
    columns = lambda v: a(v).reshape(-1, P).T
    arrays = {
        "x": a(L0_attn_x).reshape(B * L, D),
        "w_in_t": a(L0_attn_w_in).T, "w_dt_t": a(L0_attn_w_dt).T, "w_out_t": a(L0_attn_w_out).T,
        "w_cb_t": np.concatenate([a(L0_attn_w_C), a(L0_attn_w_B)]).T,
        "b_cb": np.concatenate([a(L0_attn_b_C), a(L0_attn_b_B)]),
        "b_in_c": columns(L0_attn_b_in), "b_dt_c": columns(L0_attn_b_dt), "D_c": columns(L0_attn_D),
        "A_log_c": a(L0_attn_A_log).reshape(-1, P, N).transpose(1, 0, 2),
        "b_out": L0_attn_b_out, "gamma": L0_attn_gamma, "beta": L0_attn_beta,
        "Win": L0_ffn_Win, "bin": L0_ffn_bin_, "W1": L0_ffn_W1, "b1": L0_ffn_b1, "W2": L0_ffn_W2,
        "b2": L0_ffn_b2, "Wout": L0_ffn_Wout, "bout": L0_ffn_bout,
        "c_t": a(L0_c).T.reshape(-1, P, B).transpose(1, 0, 2), "wmod": L0_wmod,
    }
    arrays = {n: np.ascontiguousarray(v) for n, v in arrays.items()}
    nc = bacc.Bacc("TRN2", target_bir_lowering=False, num_devices=1)
    ap = {n: nc.dram_tensor(f"in_{n}", v.shape, mybir.dt.from_np(v.dtype), kind="ExternalInput").ap()
          for n, v in arrays.items()}
    ap["out"] = nc.dram_tensor("out_dram", (B * L, D), mybir.dt.float32, kind="ExternalOutput").ap()
    build_program(nc, ap, B, L, D, N, M, INNER)
    r = run_bass_kernel_spmd(nc, [{f"in_{n}": v for n, v in arrays.items()}], core_ids=[0])
    return r.results[0]["out_dram"].reshape(B, L, D)
```

```python
def build_program(nc, ap, B, L, D, N, M, INNER):
    import concourse.bass as bass
    from concourse import mybir
    from contextlib import ExitStack

    f32 = mybir.dt.float32
    f32r = mybir.dt.float32r
    ALU = mybir.AluOpType
    ACT = mybir.ActivationFunctionType

    T = 128
    P = 128
    KD = D // P
    NB = L // T
    U = 64
    SU = T // U
    UNITS = KD * SU
    G = T // 32
    HN = N // 2
    J = INNER // 2
    EPS = 1e-5

    ctx = ExitStack()
    with ctx:
        def sb(name, shape, dt=f32):
            return ctx.enter_context(nc.sbuf_tensor(name, shape, dt))

        def pb(name, shape):
            return ctx.enter_context(nc.psum_tensor(name, shape, f32))

        def sem(name):
            return ctx.enter_context(nc.semaphore(name))

        w_in = sb("w_in_t", [P, KD, 2 * D])
        w_dt = sb("w_dt_t", [P, KD, D])
        w_out = sb("w_out_t", [P, KD, D])
        w_cb = sb("w_cb_t", [P, KD, 2 * N])
        win2 = sb("win2", [P, KD, 2 * M])
        ident = sb("ident", [P, P])
        mask = sb("mask", [P, 32])
        sel_c = sb("sel_c", [2 * 32, N, P], f32r)
        bias_rows = sb("bias_rows", [P, D], f32r)
        ones = sb("ones", [P, P], f32r)
        b_rep = sb("b_rep", [2 * N, G, 4, 32])
        sel_b = sb("sel_b", [2 * N, N])
        b_in = sb("b_in_col", [P, 2 * KD])
        b_dt = sb("b_dt_col", [P, KD])
        d_skip = sb("d_skip_col", [P, KD])
        b_cb = sb("b_cb_col", [2 * N, 1])
        neg_a = sb("neg_a", [P, KD, N])
        w1 = sb("w1", [P, J])
        b1 = sb("b1", [P, J])
        w2 = sb("w2", [P, J])
        b2 = sb("b2", [P, 1])
        bin2 = sb("bin2", [P, 1])
        c_t = sb("c_t", [P, KD, B])
        c_tmp = sb("c_tmp", [P, KD, B])
        mod_all = sb("mod_all", [P, 4 * KD, B])
        mod = sb("mod", [P, 4 * KD])
        gain = sb("gain", [P, D])
        shift = sb("shift", [P, D])
        wout_g = sb("wout_g", [P, D])

        x_in = sb("x_in", [P, 2, D])
        x_res = sb("x_res", [P, 2, D])
        xn = sb("xn", [P, D])
        h_t = sb("h_t", [P, 2, KD, T])
        xs_t = sb("xs_t", [P, 2, KD, T])
        sz_t = sb("sz_t", [P, 2, KD, T])
        ez = ev = sb("ez", [P, KD, T])
        v_t = u_t = sb("v_t", [P, KD, T])
        dt_t = sb("dt_t", [P, 2, KD, T])
        u_hi = sb("u_hi", [P, D], f32r)
        u_lo = sb("u_lo", [P, D], f32r)
        u_st = sb("u_st", [P, G, D], f32r)
        cb_t = sb("cb_t", [2 * N, T])
        c_st = sb("c_st", [2 * 32, T], f32r)
        b_st = sb("b_st", [P, G, N], f32r)
        b_dg = sb("b_dg", [P, 2, G, N, 32], f32r)
        c_bc = sb("c_bc", [P, 2, N, T])
        decay = sb("decay", [P, KD, SU, N, U])
        dec0 = sb("dec0", [P, SU, N])
        carry = sb("carry", [P, N])
        hs = sb("hs", [P, 4, N, U])
        state = sb("state", [P, KD, N])
        pr = sb("pr", [P, 2, N, T])
        yx = sb("yx", [P, T])
        xn2 = sb("xn2", [P, D])
        h2_t = sb("h2_t", [P, KD, T])
        rel = sb("rel", [P, J, T])
        t1 = rel[:, 0:D // T, :].rearrange("p a b -> p (a b)")
        gm = sb("gm", [P, T])
        st = [sb(f"st{n}", [P, 6]) for n in range(3)]
        mv = [sb(f"mv{n}", [P, 2]) for n in range(3)]
        lv = [sb(f"lv{n}", [P, 1]) for n in range(3)]
        rstd = [sb(f"rstd{n}", [P, 1]) for n in range(3)]
        eps = sb("eps", [P, 1])
        idle = sb("idle", [P, 1])

        work = decay[:, :, :, :, :].rearrange("p a b c d -> p (a b c d)")
        wm4 = work[:, 0:KD * 4 * D].rearrange("p (k n) -> p k n", k=KD)
        wmg = work[:, 0:KD * 2 * D].rearrange("p (k n) -> p k n", k=KD)
        row = lambda n: work[:, (2 * KD + n) * D:(2 * KD + n + 1) * D]
        gamma_b, beta_b, wout_b, bout_b, sign, gate_a, gate_b = (row(n) for n in range(7))
        c_rep = row(7).rearrange("p (k n) -> p k n", k=KD)
        b_out = x_res[0:1, 0, :]
        bout_g = sign[64:65]

        b_ps = pb("b_ps", [P, 2, N * U])
        dn = [pb(f"dense{n}", [P, 512]) for n in range(3)]
        pre_ps = dn[2]
        small = pb("small", [P, T])
        y_ps = s_ps = small[:, :]
        cb_ps = small[0:2 * N, :]
        bst_ps = small[:, 0:G * N]

        Q = 16
        N_WEIGHTS = 4 + 5 * 2 + 6
        once = """w_loaded b2_loaded wm_loaded wmg_loaded rows_loaded const_zeroed const_masks sel_copied
        neg_done scal_done c_exp c_one c_rcp silu_c mods_ps mods_done c_rep_done gates_ps sign_done gate_done
        bhi_split batch_ready""".split()
        per_block = {
            "SP": dict(ust_loaded=4 * G * Q),
            "Pool": dict(u_done=1, xres_done=1, prod_done=UNITS, tg_done=1, x1_done=1),
            "PE": dict(xt_ps=1, xs_ps=1, v_ps=1, u_ps=1, z_ps=1, cb_made=1, bst_made=1, cbc_ps=4,
                       b_ps_done=UNITS, y_ps_done=KD, res_ps=1, pre_made=1, x2t_ps=1, s_made=1, out_ps=1),
            "ACT": dict(lv0_done=1, lv1_done=1, lv2_done=1, rstd0_done=1, rstd1_done=1, rstd2_done=1,
                        h_done=KD, ab_done=1, ev_done=1, lnv_done=1, uhi_done=1, ez_done=1, lz_done=1,
                        sig_done=1, cb_done=1, cbc_done=4, dec_done=2 * KD, h2_done=KD, rel_done=J),
            "DVE": dict(st0_done=1, st1_done=1, st2_done=1, mv0_done=1, mv1_done=1, mv2_done=1, xn_done=1,
                        xs_done=1, v_done=1, dt_done=1, ulo_done=1, z_done=1, sz_done=1, chi_done=1,
                        clo_done=1, brep_done=1, bhi_done=1, blo_done=2, bdg_done=1, dec0_done=KD,
                        dec_zeroed=KD, carry_done=UNITS, b_fixed=UNITS, scan_done=UNITS, state_saved=KD,
                        pair_done=KD, yx_done=KD, yz_done=KD, t1_done=1, xn2_done=1, gm_done=J, out_done=1),
        }
        S = {n: sem(n) for n in once + [n for names in per_block.values() for n in names]}
        x_loaded = [sem("x_loaded_even"), sem("x_loaded_odd")]
        stored = [sem("stored_even"), sem("stored_odd")]

        FIRST = 4

        def count_up(eng, name):
            for n, v in per_block[name].items():
                eng.sem_inc(S[n], FIRST * v)

        def x_count(k, p):
            return k * (Q // 2) + (Q - p * (Q // 2))

        def batches(eng, start, part):
            with eng.Fori(0, B) as batch:
                start(batch)
                k = batch * NB + FIRST
                for m, on in ((-2, "e"), (-1, "ef"), (0, "efs"), (1, "efsb")):
                    part(k + m, m % 2, on)
                with eng.Fori(0, (NB - 4) // 2) as pair:
                    for m in (2, 3):
                        part(k + pair * 2 + m, m % 2, "efsbc")
                for m, on in ((-2, "fsbc"), (-1, "sbc"), (0, "bc"), (1, "c")):
                    part(k + (NB + m), m % 2, on)

        blk = ctx.enter_context(nc.Block(no_gpsimd_drain=True))

        @blk.sync
        def _(sp):
            count_up(sp, "SP")
            for n in range(2):
                sp.sem_inc(x_loaded[n], FIRST * Q // 2)
                sp.sem_inc(stored[n], FIRST * Q // 2)

            def load(dst, src):
                sp.dma_start(dst, src).then_inc(S["w_loaded"], Q)

            sp.dma_start(c_t[:, :, :], ap["c_t"]).then_inc(S["c_exp"], Q)
            load(w_in[:, :, :], ap["w_in_t"].rearrange("(k p) n -> p k n", p=P))
            load(w_dt[:, :, :], ap["w_dt_t"].rearrange("(k p) n -> p k n", p=P))
            load(w_out[:, :, :], ap["w_out_t"].rearrange("(k p) n -> p k n", p=P))
            load(w_cb[:, :, :], ap["w_cb_t"].rearrange("(k p) n -> p k n", p=P))
            for h in range(2):
                load(win2[:, :, h * M:(h + 1) * M], ap["Win"].rearrange("(k p) n -> p k n", p=P))
                load(bin2[h * M:(h + 1) * M, :], ap["bin"].rearrange("(p a) -> p a", a=1))
                for dst, src in ((w1, "W1"), (b1, "b1"), (w2, "W2")):
                    load(dst[h * M:(h + 1) * M, :], ap[src][:, h * J:(h + 1) * J])
            load(b_out, ap["b_out"].rearrange("(a n) -> a n", a=1))
            load(b_in[:, :], ap["b_in_c"])
            load(b_dt[:, :], ap["b_dt_c"])
            load(d_skip[:, :], ap["D_c"])
            load(b_cb[:, :], ap["b_cb"].rearrange("(p a) -> p a", a=1))
            load(neg_a[:, :, :], ap["A_log_c"])
            sp.wait_ge(S["const_zeroed"], 7)
            sp.dma_start(b2[0:M, :], ap["b2"].rearrange("(p a) -> p a", a=1)).then_inc(S["b2_loaded"], Q)
            sp.wait_ge(S["sel_copied"], 1)
            for n, v in enumerate((0, 1, 3, 4)):
                sp.dma_start(wm4[:, :, n * D:(n + 1) * D],
                             ap["wmod"][:, v * D:(v + 1) * D].rearrange("(k p) n -> p k n", p=P)
                             ).then_inc(S["wm_loaded"], Q)
            sp.wait_ge(S["mods_ps"], 1)

            def load_x(k, p):
                sp.dma_start(x_in[:, p, :], ap["x"][bass.ds((k - FIRST) * T, T), :]).then_inc(x_loaded[p], Q)

            def start(batch):
                k = batch * NB + FIRST
                sp.wait_ge(S["out_done"], k)
                for n, v in enumerate((2, 5)):
                    sp.dma_start(wmg[:, :, n * D:(n + 1) * D],
                                 ap["wmod"][:, v * D:(v + 1) * D].rearrange("(k p) n -> p k n", p=P)
                                 ).then_inc(S["wmg_loaded"], Q)
                for dst, src in ((gamma_b, "gamma"), (beta_b, "beta"), (bout_b, "bout")):
                    sp.dma_start(dst, ap[src].rearrange("(a n) -> a n", a=1).to_broadcast([P, D])
                                 ).then_inc(S["rows_loaded"], Q)
                for h in range(2):
                    sp.dma_start(wout_b[h * M:(h + 1) * M, :], ap["Wout"]).then_inc(S["rows_loaded"], Q)
                load_x(k, 0)
                load_x(k + 1, 1)

            def part(s, p, on):
                f, c, e = s + 1, s - 2, s + 2
                if "c" in on:
                    sp.wait_ge(S["out_done"], c + 1)
                    sp.dma_start(ap["out"][bass.ds((c - FIRST) * T, T), :], x_res[:, p, :]).then_inc(stored[p], Q)
                if "s" in on and "e" in on:
                    sp.wait_ge(S["xres_done"], s + 1)
                    load_x(e, p)
                if "f" in on:
                    for quad, (src, done) in enumerate(((u_hi, "uhi_done"), (u_hi, "uhi_done"),
                                                        (u_lo, "ulo_done"), (u_lo, "ulo_done"))):
                        sp.wait_ge(S[done], f + 1)
                        for g in range(G):
                            sp.dma_start(u_st[32 * quad:32 * quad + 32, g, :].bitcast(f32),
                                         src[32 * g:32 * g + 32, :].bitcast(f32)).then_inc(S["ust_loaded"], Q)

            batches(sp, start, part)
            for n in range(2):
                sp.wait_ge(stored[n], (B * NB + FIRST) * Q // 2)

        @blk.gpsimd
        def _(gp):
            count_up(gp, "Pool")
            f_sel = work[0:64, 0:N * P].rearrange("p (n c) -> p n c", n=N)
            for t, v in ((ident, 0.0), (mask, 0.0), (sel_b, 0.0), (ones, 1.0), (bias_rows, 0.0), (b2, 0.0)):
                gp.memset(t[:, :].bitcast(f32), v).then_inc(S["const_zeroed"], 1)
            gp.memset(f_sel, 0.0).then_inc(S["const_zeroed"], 1)
            gp.wait_ge(S["const_zeroed"], 7)

            def select(view, base, pattern, n):
                gp.affine_select(out=view, in_=view, compare_op=ALU.not_equal, fill=1.0, base=base,
                                 pattern=pattern, channel_multiplier=1).then_inc(S["const_masks"], 1)
                gp.wait_ge(S["const_masks"], n)

            select(ident[:, :], 0, [[-1, P]], 1)
            for q in range(4):
                select(mask[:, :], -32 * q, [[-1, 32]], 2 + q)
            select(sel_b[:, :], -N, [[-1, N]], 6)
            for q in range(2):
                select(f_sel, -32 * q, [[-1, N], [0, P]], 7 + q)

            def start(batch):
                gp.wait_ge(S["batch_ready"], batch + 1)

            def part(s, p, on):
                f, b, q = s + 1, s - 1, 1 - p
                for u in range(UNITS):
                    j, half = u // SU, u % SU
                    if u == 6 and "f" in on:
                        gp.wait_ge(S["dt_done"], f + 1)
                        gp.wait_ge(S["u_ps"], f)
                        gp.tensor_tensor(u_t[:, :, :], dt_t[:, q, :, :], xs_t[:, q, :, :], ALU.mult
                                         ).then_inc(S["u_done"], 1)
                    if "s" in on:
                        gp.wait_ge(S["scan_done"], s * UNITS + (u + 1))
                        if u == 0:
                            gp.wait_ge(S["cbc_done"], s * 4 + 4)
                        if half == 0:
                            gp.wait_ge(S["y_ps_done"], s * KD + (j - 1))
                        gp.tensor_tensor(pr[:, j % 2, :, half * U:(half + 1) * U], hs[:, u % 4, :, :],
                                         c_bc[:, p, :, half * U:(half + 1) * U], ALU.mult
                                         ).then_inc(S["prod_done"], 1)
                    if u == 3 and "s" in on:
                        gp.wait_ge(x_loaded[p], x_count(s, p))
                        gp.wait_ge(stored[p], x_count(s - 2, p))
                        gp.tensor_tensor(x_res[:, p, :], x_in[:, p, :], shift[:, :], ALU.add
                                         ).then_inc(S["xres_done"], 1)
                    if u == 4 and "b" in on:
                        gp.wait_ge(S["t1_done"], b + 1)
                        gp.tensor_tensor(t1, t1, gain[:, :], ALU.mult).then_inc(S["tg_done"], 1)
                        gp.wait_ge(S["tg_done"], b + 1)
                        gp.tensor_tensor(x_res[:, q, :], x_res[:, q, :], t1, ALU.add
                                         ).then_inc(S["x1_done"], 1)

            batches(gp, start, part)

        @blk.tensor
        def _(pe):
            count_up(pe, "PE")
            mm = nc.tensor.matmul
            pe.wait_ge(S["w_loaded"], Q * N_WEIGHTS)
            pe.wait_ge(S["const_masks"], 8)
            pe.wait_ge(S["silu_c"], 1)
            pe.wait_ge(S["wm_loaded"], Q * 4)
            for m in range(4 * KD):
                for j in range(KD):
                    last = mm(dn[0][:, m * B:(m + 1) * B], wm4[:, j, m * P:(m + 1) * P], c_t[:, j, :],
                              start=(j == 0), stop=(j == KD - 1))
            last.then_inc(S["mods_ps"], 1)
            pe.wait_ge(S["mods_done"], 2)

            def start(batch):
                pe.wait_ge(S["c_rep_done"], batch + 1)
                pe.wait_ge(S["wmg_loaded"], batch * (2 * Q) + 2 * Q)
                pe.wait_ge(S["out_done"], batch * NB + FIRST)
                for n in range(2):
                    for j in range(KD):
                        last = mm(dn[n][:, :], c_rep[:, j, :], wmg[:, j, n * D:(n + 1) * D],
                                  start=(j == 0), stop=(j == KD - 1))
                last.then_inc(S["gates_ps"], 1)
                pe.wait_ge(S["batch_ready"], batch + 1)

            def scan_input(s, p, u):
                j, half = u // SU, u % SU
                if u == 0:
                    pe.wait_ge(S["bdg_done"], s + 1)
                    pe.wait_ge(S["ust_loaded"], s * (4 * G * Q) + 4 * G * Q)
                pe.wait_ge(S["scan_done"], s * UNITS + (u - 1))
                for g in range(2):
                    for h in range(2):
                        bank = b_ps[:, u % 2, h * 512:(h + 1) * 512].rearrange("p (n t) -> p n t", t=U)
                        last = mm(bank[:, :, g * 32:(g + 1) * 32],
                                  u_st[:, 2 * half + g, j * P:(j + 1) * P],
                                  b_dg[:, p, 2 * half + g, h * HN:(h + 1) * HN, :], start=True, stop=True)
                last.then_inc(S["b_ps_done"], 1)

            def sum_states(s, j):
                pe.wait_ge(S["pair_done"], s * KD + (j + 1))
                pe.wait_ge(S["yx_done"], s * KD + j)
                for n in range(HN):
                    last = mm(y_ps, ident[:, :], pr[:, j % 2, n, :], start=(n == 0),
                              stop=(n == HN - 1))
                last.then_inc(S["y_ps_done"], 1)

            def transpose4(dst, src, ready):
                for j in range(KD):
                    last = nc.tensor.transpose(dst[:, j * P:(j + 1) * P], src[:, j * P:(j + 1) * P], ident[:, :])
                last.then_inc(ready, 1)

            def project(dst, w, col, src, ready):
                for m in range(KD):
                    for j in range(KD):
                        last = mm(dst[:, m * T:(m + 1) * T], w[:, j, col + m * P:col + (m + 1) * P], src[:, j, :],
                                  start=(j == 0), stop=(j == KD - 1))
                last.then_inc(ready, 1)

            def part(s, p, on):
                f, b, c, q = s + 1, s - 1, s - 2, 1 - p
                for u in range(UNITS):
                    if u > 0 and u + 1 < UNITS and "s" in on:
                        scan_input(s, p, u + 1)
                    if u == 0:
                        if "c" in on:
                            pe.wait_ge(S["h2_done"], c * KD + KD)
                            if "b" in on:
                                pe.wait_ge(S["yx_done"], b * KD + 3)
                            for j in range(KD):
                                last = mm(s_ps, win2[:, j, :], h2_t[:, j, :], start=(j == 0), stop=(j == KD - 1))
                            last.then_inc(S["s_made"], 1)
                        if "f" in on:
                            pe.wait_ge(S["cbc_done"], f * 4)
                            pe.wait_ge(S["xn_done"], f + 1)
                            transpose4(dn[1], xn, S["xt_ps"])
                        if "s" in on:
                            pe.wait_ge(S["cbc_done"], s * 4 + 3)
                            pe.wait_ge(S["h2_done"], (s - 1) * KD)
                            project(dn[0], w_in, D, h_t[:, p, :, :], S["z_ps"])
                            scan_input(s, p, 0)
                            scan_input(s, p, 1)
                    if u == 1 and "b" in on:
                        pe.wait_ge(S["rel_done"], b * J)
                        sum_states(b, KD - 1)
                    if u == 2:
                        if "f" in on:
                            pe.wait_ge(S["h_done"], f * KD + KD)
                            project(dn[1], w_in, 0, h_t[:, q, :, :], S["xs_ps"])
                        if "c" in on:
                            if "s" in on:
                                pe.wait_ge(S["z_done"], s + 1)
                            pe.wait_ge(S["gm_done"], c * J + J)
                            mm(dn[0][:, :], ones[64:P, :], bias_rows[64:P, :], start=True, stop=False)
                            mm(dn[0][:, :], gm[:, :], wout_g[:, :], start=False, stop=True
                               ).then_inc(S["out_ps"], 1)
                    if u == 3:
                        if "s" in on:
                            sum_states(s, 0)
                        if "b" in on:
                            pe.wait_ge(S["yz_done"], b * KD + KD)
                            for j in range(KD):
                                last = mm(pre_ps[:, :], sz_t[:, q, j, :], w_out[:, j, :], start=False,
                                          stop=(j == KD - 1))
                            last.then_inc(S["pre_made"], 1)
                    if u == 4 and "f" in on:
                        pe.wait_ge(S["xs_done"], f + 1)
                        if "c" in on:
                            pe.wait_ge(S["out_done"], c + 1)
                        if "s" in on:
                            pe.wait_ge(S["z_done"], s + 1)
                        project(dn[0], w_dt, 0, xs_t[:, q, :, :], S["v_ps"])
                        if "s" in on:
                            pe.wait_ge(S["yx_done"], s * KD + 1)
                        for j in range(KD):
                            last = mm(cb_ps, w_cb[:, j, :], xs_t[:, q, j, :], start=(j == 0), stop=(j == KD - 1))
                        last.then_inc(S["cb_made"], 1)
                    if u == 5 and "s" in on:
                        if "f" in on:
                            pe.wait_ge(S["cb_done"], f + 1)
                        sum_states(s, 1)
                    if u == 6 and "f" in on:
                        if "s" in on:
                            pe.wait_ge(S["yx_done"], s * KD + 2)
                        pe.wait_ge(S["brep_done"], f + 1)
                        for g in range(G):
                            last = mm(bst_ps[:, g * N:(g + 1) * N], b_rep[:, g, :, :].rearrange("p a b -> p (a b)"),
                                      sel_b[:, :], start=True, stop=True)
                        last.then_inc(S["bst_made"], 1)
                        pe.wait_ge(S["t1_done"], f - 1)
                        pe.wait_ge(S["u_done"], f + 1)
                        transpose4(pre_ps, u_t[:, :, :].rearrange("p a b -> p (a b)"), S["u_ps"])
                        pe.wait_ge(S["clo_done"], f + 1)
                        pe.wait_ge(S["v_done"], f + 1)
                        for n4 in range(4):
                            if n4 >= 2:
                                pe.wait_ge(S["cbc_done"], f * 4 + (n4 - 1))
                            for n in range(4):
                                last = mm(dn[n4 % 2][:, n * T:(n + 1) * T], sel_c[:, 4 * n4 + n, :], c_st[:, :],
                                          start=True, stop=True)
                            last.then_inc(S["cbc_ps"], 1)
                    if u == 7:
                        if "b" in on:
                            if "f" in on:
                                pe.wait_ge(S["cbc_done"], f * 4 + 3)
                            elif "s" in on:
                                pe.wait_ge(S["z_done"], s + 1)
                            if "c" in on:
                                pe.wait_ge(S["out_done"], c + 1)
                            pe.wait_ge(S["xn2_done"], b + 1)
                            transpose4(dn[0], xn2, S["x2t_ps"])
                        if "s" in on:
                            if "f" in on:
                                pe.wait_ge(S["blo_done"], f * 2 + 2)
                            sum_states(s, 2)
                        if "s" in on:
                            if "f" in on:
                                pe.wait_ge(S["ulo_done"], f + 1)
                            pe.wait_ge(S["t1_done"], s)
                            mm(pre_ps[:, :], ones[0:64, :], bias_rows[0:64, :], start=True, stop=False)
                            for j in range(KD):
                                last = mm(pre_ps[:, j * P:(j + 1) * P], h_t[:, p, j, :], ident[:, :], start=False,
                                          stop=False)
                            last.then_inc(S["res_ps"], 1)

            batches(pe, start, part)

        @blk.scalar
        def _(act):
            count_up(act, "ACT")
            A = nc.scalar.activation
            nc.scalar.preload_act_table_set("natural_log_exp_and_others")
            act.wait_ge(S["c_exp"], Q)
            A(c_tmp[:, :, :], c_t[:, :, :], ACT.Exp, scale=-1.0).then_inc(S["c_exp"], 1)
            act.wait_ge(S["w_loaded"], Q * N_WEIGHTS)
            A(neg_a[:, :, :], neg_a[:, :, :], ACT.Exp).then_inc(S["neg_done"], 1)

            def start(batch):
                act.wait_ge(S["scal_done"], 1)
                act.wait_ge(S["batch_ready"], batch + 1)

            def decays(k, p, j, h):
                if h == 0:
                    if j == 0:
                        act.wait_ge(S["dt_done"], k + 1)
                    act.wait_ge(S["scan_done"], k * UNITS + (SU * (j + 1) - UNITS))
                for n in range(h * HN, (h + 1) * HN):
                    last = A(decay[:, j, :, n, :], dt_t[:, p, j, :].rearrange("p (s t) -> p s t", s=SU), ACT.Exp,
                             scale=neg_a[:, j, n:n + 1])
                last.then_inc(S["dec_done"], 1)

            def inv_std(n, k):
                act.wait_ge(S[f"mv{n}_done"], k + 1)
                A(lv[n][:, :], mv[n][:, 1:2], ACT.Ln, bias=eps[:, :]).then_inc(S[f"lv{n}_done"], 1)
                act.wait_ge(S[f"lv{n}_done"], k + 1)
                A(rstd[n][:, :], lv[n][:, :], ACT.Exp, scale=-0.5).then_inc(S[f"rstd{n}_done"], 1)

            def modulate(dst, psum, done, scale, shift_):
                for j in range(KD):
                    A(dst[:, j, :], psum[:, j * T:(j + 1) * T], ACT.Identity, scale=mod[:, scale + j:scale + j + 1],
                      bias=mod[:, shift_ + j:shift_ + j + 1]).then_inc(done, 1)

            def part(s, p, on):
                f, b, c, e, q = s + 1, s - 1, s - 2, s + 2, 1 - p
                for u in range(UNITS):
                    if u == 0 and "c" in on:
                        act.wait_ge(S["s_made"], c + 1)
                        act.wait_ge(S["gm_done"], c * J)
                        act.wait_ge(S["x1_done"], c + 1)
                        for j in range(J):
                            A(rel[:, j, :], s_ps, ACT.Relu, scale=w1[:, j:j + 1], bias=b1[:, j:j + 1]
                              ).then_inc(S["rel_done"], 1)
                    if u == 0 and "f" in on:
                        act.wait_ge(S["xt_ps"], f + 1)
                        act.wait_ge(S["res_ps"], f - 1)
                        modulate(h_t[:, q, :, :], dn[1], S["h_done"], KD, 0)
                    if "s" in on:
                        for half_tile in {0: (2,), 1: (3, 4), 2: (5,), 3: (6, 7)}.get(u, ()):
                            decays(s, p, half_tile // 2, half_tile % 2)
                    if u == 2 and "s" in on:
                        act.wait_ge(S["z_done"], s + 1)
                        act.wait_ge(S["dt_done"], s + 1)
                        A(ez[:, :, :], sz_t[:, p, :, :], ACT.Exp, scale=-1.0).then_inc(S["ez_done"], 1)
                        act.wait_ge(S["ez_done"], s + 1)
                        A(ez[:, :, :], ez[:, :, :], ACT.Ln, bias=1.0).then_inc(S["lz_done"], 1)
                        act.wait_ge(S["lz_done"], s + 1)
                        A(ez[:, :, :], ez[:, :, :], ACT.Exp, scale=-1.0).then_inc(S["sig_done"], 1)
                    if u == 4 and "b" in on:
                        inv_std(1, b)
                    if u == 5 and "f" in on:
                        act.wait_ge(S["cb_made"], f + 1)
                        act.wait_ge(S["brep_done"], f)
                        A(cb_t[:, :], cb_ps, ACT.Identity, bias=b_cb[:, :]).then_inc(S["cb_done"], 1)
                        act.wait_ge(S["v_done"], f + 1)
                        act.wait_ge(S["sz_done"], f)
                        A(ev[:, :, :], v_t[:, :, :], ACT.Abs).then_inc(S["ab_done"], 1)
                        act.wait_ge(S["ab_done"], f + 1)
                        A(ev[:, :, :], ev[:, :, :], ACT.Exp, scale=-1.0).then_inc(S["ev_done"], 1)
                        act.wait_ge(S["ev_done"], f + 1)
                        A(ev[:, :, :], ev[:, :, :], ACT.Ln, bias=1.0).then_inc(S["lnv_done"], 1)
                    if u == 6 and "b" in on:
                        inv_std(2, b)
                    if u == 6 and "f" in on:
                        decays(f, q, 0, 0)
                    if u == 6 and "e" in on:
                        inv_std(0, e)
                    if u == 6 and "f" in on:
                        act.wait_ge(S["prod_done"], f * UNITS - UNITS)
                        for n4 in range(4):
                            act.wait_ge(S["cbc_ps"], f * 4 + (n4 + 1))
                            A(c_bc[:, q, 4 * n4:4 * n4 + 4, :], dn[n4 % 2][:, :].rearrange("p (n t) -> p n t", n=4),
                              ACT.Copy).then_inc(S["cbc_done"], 1)
                            if n4 == 0:
                                act.wait_ge(S["u_ps"], f + 1)
                                act.wait_ge(S["ust_loaded"], f * (4 * G * Q))
                                act.wait_ge(S["b_ps_done"], f * UNITS)
                                A(u_hi[:, :], pre_ps[:, :], ACT.Copy).then_inc(S["uhi_done"], 1)
                    if u == 7 and "b" in on:
                        act.wait_ge(S["x2t_ps"], b + 1)
                        act.wait_ge(S["s_made"], b)
                        modulate(h2_t, dn[0], S["h2_done"], 3 * KD, 2 * KD)
                    if u == 7 and "f" in on:
                        decays(f, q, 0, 1)

            batches(act, start, part)

        @blk.vector
        def _(dve):
            count_up(dve, "DVE")
            V = nc.vector
            dve.wait_ge(S["const_masks"], 8)
            V.tensor_copy(sel_c[:, :, :], work[0:64, 0:N * P].rearrange("p (n c) -> p n c", n=N)
                          ).then_inc(S["sel_copied"], 1)
            V.memset(eps[:, :], EPS)
            dve.wait_ge(S["c_exp"], Q + 1)
            V.tensor_scalar(c_tmp[:, :, :], c_tmp[:, :, :], 1.0, None, ALU.add).then_inc(S["c_one"], 1)
            dve.wait_ge(S["c_one"], 1)
            V.reciprocal(c_tmp[:, :, :], c_tmp[:, :, :]).then_inc(S["c_rcp"], 1)
            dve.wait_ge(S["c_rcp"], 1)
            V.tensor_tensor(c_t[:, :, :], c_t[:, :, :], c_tmp[:, :, :], ALU.mult).then_inc(S["silu_c"], 1)
            dve.wait_ge(S["neg_done"], 1)
            V.tensor_scalar(neg_a[:, :, :], neg_a[:, :, :], -1.0, None, ALU.mult)
            dve.wait_ge(S["w_loaded"], Q * N_WEIGHTS)
            dve.wait_ge(S["b2_loaded"], Q)
            V.scalar_tensor_tensor(b1[:, :], w1[:, :], bin2[:, :], b1[:, :], ALU.mult, ALU.add
                                   ).then_inc(S["scal_done"], 1)
            V.tensor_copy(bias_rows[0:1, :], b_out).then_inc(S["bhi_split"], 1)
            dve.wait_ge(S["bhi_split"], 1)
            V.tensor_tensor(bias_rows[32:33, :], b_out, bias_rows[0:1, :].bitcast(f32), ALU.subtract)
            dve.wait_ge(S["mods_ps"], 1)
            for n, plus in enumerate((0.0, 1.0, 0.0, 1.0)):
                last = V.tensor_scalar(mod_all[:, n * KD:(n + 1) * KD, :],
                                       dn[0][:, n * KD * B:(n + 1) * KD * B].rearrange("p (m b) -> p m b", b=B),
                                       plus, None, ALU.add)
            last.then_inc(S["mods_done"], 2)

            def start(batch):
                dve.wait_ge(S["mods_done"], 2)
                dve.wait_ge(S["silu_c"], 1)
                V.tensor_copy(c_rep[:, :, :], c_t[:, :, bass.ds(batch, 1)].to_broadcast([P, KD, P])
                              ).then_inc(S["c_rep_done"], 1)
                V.tensor_copy(mod[:, :], mod_all[:, :, bass.ds(batch, 1)].rearrange("p m b -> p (m b)"))
                V.memset(state[:, :, :], 0.0)
                dve.wait_ge(S["rows_loaded"], batch * (5 * Q) + 5 * Q)
                dve.wait_ge(S["gates_ps"], batch + 1)
                for n, gate in enumerate((gate_a, gate_b)):
                    V.tensor_scalar(sign, dn[n][:, :], 0.0, 2.0, ALU.is_ge, ALU.mult).then_inc(S["sign_done"], 1)
                    dve.wait_ge(S["sign_done"], batch * 6 + (3 * n + 1))
                    V.tensor_scalar(sign, sign, -1.0, None, ALU.add).then_inc(S["sign_done"], 1)
                    dve.wait_ge(S["sign_done"], batch * 6 + (3 * n + 2))
                    V.tensor_tensor(gate, sign, dn[n][:, :], ALU.mult).then_inc(S["sign_done"], 1)
                    dve.wait_ge(S["sign_done"], batch * 6 + (3 * n + 3))
                    V.scalar_tensor_tensor(gate, gate, 0.25, sign, ALU.max, ALU.mult).then_inc(S["gate_done"], 1)
                    dve.wait_ge(S["gate_done"], batch * 2 + (n + 1))
                V.tensor_tensor(gain[:, :], gate_a, gamma_b, ALU.mult)
                V.tensor_tensor(shift[:, :], gate_a, beta_b, ALU.mult)
                V.tensor_tensor(wout_g[:, :], gate_b, wout_b, ALU.mult)
                V.tensor_tensor(bout_g, gate_b[64:65, :], bout_b[64:65, :], ALU.mult
                                ).then_inc(S["bhi_split"], 1)
                dve.wait_ge(S["bhi_split"], batch * 2 + 2)
                V.tensor_copy(bias_rows[64:65, :], bout_g).then_inc(S["bhi_split"], 1)
                dve.wait_ge(S["bhi_split"], batch * 2 + 3)
                V.tensor_tensor(bias_rows[96:97, :], bout_g, bias_rows[64:65, :].bitcast(f32), ALU.subtract
                                ).then_inc(S["batch_ready"], 1)
                dve.wait_ge(S["batch_ready"], batch + 1)

            def scan_unit(s, p, u):
                j, half = u // SU, u % SU
                if half == 0:
                    dve.wait_ge(S["dec_done"], s * (2 * KD) + (2 * j + 2))
                    V.tensor_copy(dec0[:, :, :], decay[:, j, :, :, 0]).then_inc(S["dec0_done"], 1)
                    dve.wait_ge(S["dec0_done"], s * KD + (j + 1))
                    V.memset(decay[:, j, :, :, 0], 0.0).then_inc(S["dec_zeroed"], 1)
                    dve.wait_ge(S["state_saved"], s * KD + (j + 1 - KD))
                    before = state[:, j, :]
                else:
                    before = hs[:, (u - 1) % 4, :, U - 1]
                    dve.wait_ge(S["scan_done"], s * UNITS + u)
                V.tensor_tensor(carry[:, :], dec0[:, half, :], before, ALU.mult).then_inc(S["carry_done"], 1)
                dve.wait_ge(S["carry_done"], s * UNITS + (u + 1))
                dve.wait_ge(S["b_ps_done"], s * UNITS + (u + 1))
                inputs = b_ps[:, u % 2, :]
                heads = inputs.rearrange("p (n t) -> p n t", t=U)[:, :, 0]
                V.tensor_tensor(heads, heads, carry[:, :], ALU.add).then_inc(S["b_fixed"], 1)
                dve.wait_ge(S["b_fixed"], s * UNITS + (u + 1))
                dve.wait_ge(S["dec_zeroed"], s * KD + (j + 1))
                dve.wait_ge(S["prod_done"], s * UNITS + (u - 3))
                V.tensor_tensor_scan(hs[:, u % 4, :, :].rearrange("p n t -> p (n t)"),
                                     decay[:, j, half, :, :].rearrange("p n t -> p (n t)"), inputs, 0.0,
                                     ALU.mult, ALU.add).then_inc(S["scan_done"], 1)
                if half == SU - 1:
                    dve.wait_ge(S["scan_done"], s * UNITS + (u + 1))
                    V.tensor_copy(state[:, j, :], hs[:, u % 4, :, U - 1]).then_inc(S["state_saved"], 1)

            def add_pairs(s, j):
                dve.wait_ge(S["prod_done"], s * UNITS + SU * (j + 1))
                V.tensor_tensor(pr[:, j % 2, 0:HN, :], pr[:, j % 2, 0:HN, :], pr[:, j % 2, HN:N, :], ALU.add
                                ).then_inc(S["pair_done"], 1)

            def gate_y(s, p, j):
                dve.wait_ge(S["yz_done"], s * KD + j)
                dve.wait_ge(S["y_ps_done"], s * KD + (j + 1))
                V.scalar_tensor_tensor(yx[:, :], xs_t[:, p, j, :], d_skip[:, j:j + 1], y_ps,
                                       ALU.mult, ALU.add).then_inc(S["yx_done"], 1)
                dve.wait_ge(S["yx_done"], s * KD + (j + 1))
                V.tensor_tensor(sz_t[:, p, j, :], sz_t[:, p, j, :], yx[:, :], ALU.mult).then_inc(S["yz_done"], 1)

            def moments(n, k, src):
                V.bn_stats(st[n][:, :], src).then_inc(S[f"st{n}_done"], 1)
                dve.wait_ge(S[f"st{n}_done"], k + 1)
                V.memset(idle[:, :], 0.0)
                V.bn_aggr(mv[n][:, :], st[n][:, :]).then_inc(S[f"mv{n}_done"], 1)

            def normalize(n, k, dst, src, done):
                dve.wait_ge(S[f"rstd{n}_done"], k + 1)
                V.tensor_scalar(dst, src, mv[n][:, 0:1], rstd[n][:, :], ALU.subtract, ALU.mult).then_inc(done, 1)

            def bias4(dst, psum, bias, done):
                V.tensor_tensor(dst, psum[:, :].rearrange("p (k t) -> p k t", k=KD),
                                bias.unsqueeze(2).to_broadcast([P, KD, T]), ALU.add).then_inc(done, 1)

            def part(s, p, on):
                f, b, c, e, q = s + 1, s - 1, s - 2, s + 2, 1 - p
                for u in range(UNITS):
                    if u == 0 and "b" in on:
                        gate_y(b, q, 2)
                        add_pairs(b, KD - 1)
                    if u == 0 and "c" in on:
                        dve.wait_ge(S["rel_done"], c * J + 1)
                        dve.wait_ge(S["out_ps"], c)
                        V.tensor_scalar(gm[:, :], rel[:, 0, :], w2[:, 0:1], b2[:, :], ALU.mult, ALU.add
                                        ).then_inc(S["gm_done"], 1)
                        for j in range(1, J):
                            dve.wait_ge(S["gm_done"], c * J + j)
                            dve.wait_ge(S["rel_done"], c * J + (j + 1))
                            V.scalar_tensor_tensor(gm[:, :], rel[:, j, :], w2[:, j:j + 1], gm[:, :], ALU.mult,
                                                   ALU.add).then_inc(S["gm_done"], 1)
                    if u == 1 and "s" in on:
                        dve.wait_ge(S["z_ps"], s + 1)
                        bias4(sz_t[:, p, :, :], dn[0], b_in[:, KD:2 * KD], S["z_done"])
                    if u == 2 and "b" in on:
                        gate_y(b, q, 3)
                    if u == 3 and "f" in on:
                        dve.wait_ge(S["xs_ps"], f + 1)
                        bias4(xs_t[:, q, :, :], dn[1], b_in[:, 0:KD], S["xs_done"])
                    if u == 4 and "s" in on:
                        gate_y(s, p, 0)
                    if u == 5 and "f" in on:
                        dve.wait_ge(S["v_ps"], f + 1)
                        dve.wait_ge(S["u_ps"], f)
                        bias4(v_t[:, :, :], dn[0], b_dt[:, :], S["v_done"])
                    if u == 6 and "s" in on:
                        gate_y(s, p, 1)
                    if u == 6 and "f" in on:
                        dve.wait_ge(S["cb_done"], f + 1)
                        dve.wait_ge(S["cbc_ps"], f * 4)
                        V.tensor_copy(c_st[0:32, :], cb_t[:, :]).then_inc(S["chi_done"], 1)
                        dve.wait_ge(S["bst_made"], f)
                        V.tensor_copy(b_rep[:, :, :, :],
                                      cb_t[:, :].rearrange("p (g o t) -> p g o t", g=G, o=1
                                                           ).to_broadcast([2 * N, G, 4, 32])
                                      ).then_inc(S["brep_done"], 1)
                        dve.wait_ge(S["chi_done"], f + 1)
                        V.tensor_tensor(c_st[32:64, :], cb_t[:, :], c_st[0:32, :].bitcast(f32), ALU.subtract
                                        ).then_inc(S["clo_done"], 1)
                    if u == 6 and "b" in on:
                        dve.wait_ge(S["x2t_ps"], b)
                        normalize(2, b, xn2[:, :], x_res[:, q, :], S["xn2_done"])
                    if u == 6 and "e" in on:
                        dve.wait_ge(x_loaded[p], x_count(e, p))
                        moments(0, e, x_in[:, p, :])
                    if u == 7 and "e" in on:
                        dve.wait_ge(S["xt_ps"], e)
                        normalize(0, e, xn[:, :], x_in[:, p, :], S["xn_done"])
                    if "s" in on:
                        scan_unit(s, p, u)
                    if u in (2, 4, 6) and "s" in on:
                        add_pairs(s, u // 2 - 1)
                    if u == 3 and "c" in on:
                        dve.wait_ge(S["out_ps"], c + 1)
                        V.tensor_tensor(x_res[:, p, :], x_res[:, p, :], dn[0][:, :], ALU.add
                                        ).then_inc(S["out_done"], 1)
                    if u == 3 and "s" in on:
                        dve.wait_ge(S["sig_done"], s + 1)
                        V.tensor_tensor(sz_t[:, p, :, :], sz_t[:, p, :, :], ez[:, :, :], ALU.mult
                                        ).then_inc(S["sz_done"], 1)
                        dve.wait_ge(S["sz_done"], s + 1)
                    if u == 4 and "b" in on:
                        dve.wait_ge(S["pre_made"], b + 1)
                        moments(1, b, pre_ps[:, :])
                        normalize(1, b, t1, pre_ps[:, :], S["t1_done"])
                    if u == 5 and "f" in on:
                        dve.wait_ge(S["lnv_done"], f + 1)
                        V.scalar_tensor_tensor(dt_t[:, q, :, :].rearrange("p k t -> p (k t)"),
                                               v_t[:, :, :].rearrange("p k t -> p (k t)"), 0.0,
                                               ev[:, :, :].rearrange("p k t -> p (k t)"), ALU.max, ALU.add
                                               ).then_inc(S["dt_done"], 1)
                    if u == 5 and "b" in on:
                        dve.wait_ge(S["x1_done"], b + 1)
                        moments(2, b, x_res[:, q, :])
                    if u == 6 and "f" in on:
                        dve.wait_ge(S["bst_made"], f + 1)
                        dve.wait_ge(S["bdg_done"], f)
                        src = bst_ps.rearrange("p (g n) -> p g n", g=G)
                        V.tensor_copy(b_st[:, :, :], src).then_inc(S["bhi_done"], 1)
                        dve.wait_ge(S["bhi_done"], f + 1)
                        for quad in (1, 3):
                            rows = slice(32 * quad, 32 * quad + 32)
                            V.tensor_tensor(b_st[rows, :, :], src[rows], b_st[rows, :, :].bitcast(f32),
                                            ALU.subtract).then_inc(S["blo_done"], 1)
                        dve.wait_ge(S["blo_done"], f * 2 + 2)
                        dve.wait_ge(S["uhi_done"], f + 1)
                        V.tensor_tensor(u_lo[:, :], pre_ps[:, :], u_hi[:, :].bitcast(f32), ALU.subtract
                                        ).then_inc(S["ulo_done"], 1)
                        for g in range(G):
                            last = V.tensor_tensor(
                                b_dg[:, q, g, :, :], mask[:, :].unsqueeze(1).to_broadcast([P, N, 32]),
                                b_st[:, g, :].bitcast(f32).unsqueeze(2).to_broadcast([P, N, 32]), ALU.mult)
                        last.then_inc(S["bdg_done"], 1)

            batches(dve, start, part)


def kernel(L0_attn_x, L0_attn_w_in, L0_attn_b_in, L0_attn_w_dt, L0_attn_b_dt, L0_attn_A_log, L0_attn_w_B,
           L0_attn_b_B, L0_attn_w_C, L0_attn_b_C, L0_attn_D, L0_attn_w_out, L0_attn_b_out, L0_attn_gamma,
           L0_attn_beta, L0_ffn_Win, L0_ffn_bin_, L0_ffn_W1, L0_ffn_b1, L0_ffn_W2, L0_ffn_b2, L0_ffn_Wout,
           L0_ffn_bout, L0_c, L0_wmod):
    import numpy as np
    import concourse.bacc as bacc
    from concourse import mybir
    from concourse.bass_utils import run_bass_kernel_spmd

    B, L, D = L0_attn_x.shape
    N = L0_attn_A_log.shape[1]
    M, INNER = L0_ffn_W1.shape
    P = 128
    a = np.asarray
    columns = lambda v: a(v).reshape(-1, P).T
    arrays = {
        "x": a(L0_attn_x).reshape(B * L, D),
        "w_in_t": a(L0_attn_w_in).T, "w_dt_t": a(L0_attn_w_dt).T, "w_out_t": a(L0_attn_w_out).T,
        "w_cb_t": np.concatenate([a(L0_attn_w_C), a(L0_attn_w_B)]).T,
        "b_cb": np.concatenate([a(L0_attn_b_C), a(L0_attn_b_B)]),
        "b_in_c": columns(L0_attn_b_in), "b_dt_c": columns(L0_attn_b_dt), "D_c": columns(L0_attn_D),
        "A_log_c": a(L0_attn_A_log).reshape(-1, P, N).transpose(1, 0, 2),
        "b_out": L0_attn_b_out, "gamma": L0_attn_gamma, "beta": L0_attn_beta,
        "Win": L0_ffn_Win, "bin": L0_ffn_bin_, "W1": L0_ffn_W1, "b1": L0_ffn_b1, "W2": L0_ffn_W2,
        "b2": L0_ffn_b2, "Wout": L0_ffn_Wout, "bout": L0_ffn_bout,
        "c_t": a(L0_c).T.reshape(-1, P, B).transpose(1, 0, 2), "wmod": L0_wmod,
    }
    arrays = {n: np.ascontiguousarray(v) for n, v in arrays.items()}
    nc = bacc.Bacc("TRN2", target_bir_lowering=False, num_devices=1)
    ap = {n: nc.dram_tensor(f"in_{n}", v.shape, mybir.dt.from_np(v.dtype), kind="ExternalInput").ap()
          for n, v in arrays.items()}
    ap["out"] = nc.dram_tensor("out_dram", (B * L, D), mybir.dt.float32, kind="ExternalOutput").ap()
    build_program(nc, ap, B, L, D, N, M, INNER)
    r = run_bass_kernel_spmd(nc, [{f"in_{n}": v for n, v in arrays.items()}], core_ids=[0])
    return r.results[0]["out_dram"].reshape(B, L, D)
```

```python
def build_program(nc, ap, B, L, D, N, M, INNER):
    import concourse.bass as bass
    from concourse import mybir
    from contextlib import ExitStack

    f32 = mybir.dt.float32
    f32r = mybir.dt.float32r
    ALU = mybir.AluOpType
    ACT = mybir.ActivationFunctionType

    T = 128
    P = 128
    KD = D // P
    NB = L // T
    U = 64
    SU = T // U
    UNITS = KD * SU
    G = T // 32
    HN = N // 2
    J = INNER // 2
    EPS = 1e-5

    ctx = ExitStack()
    with ctx:
        def sb(name, shape, dt=f32):
            return ctx.enter_context(nc.sbuf_tensor(name, shape, dt))

        def pb(name, shape):
            return ctx.enter_context(nc.psum_tensor(name, shape, f32))

        def sem(name):
            return ctx.enter_context(nc.semaphore(name))

        w_in = sb("w_in_t", [P, KD, 2 * D])
        w_dt = sb("w_dt_t", [P, KD, D])
        w_out = sb("w_out_t", [P, KD, D])
        w_cb = sb("w_cb_t", [P, KD, 2 * N])
        win2 = sb("win2", [P, KD, 2 * M])
        ident = sb("ident", [P, P])
        mask = sb("mask", [P, 32])
        sel_c = sb("sel_c", [2 * 32, N, P], f32r)
        bias_rows = sb("bias_rows", [P, D], f32r)
        ones = sb("ones", [P, P], f32r)
        b_rep = sb("b_rep", [2 * N, G, 4, 32])
        sel_b = sb("sel_b", [2 * N, N])
        b_in = sb("b_in_col", [P, 2 * KD])
        b_dt = sb("b_dt_col", [P, KD])
        d_skip = sb("d_skip_col", [P, KD])
        b_cb = sb("b_cb_col", [2 * N, 1])
        neg_a = sb("neg_a", [P, KD, N])
        w1 = sb("w1", [P, J])
        b1 = sb("b1", [P, J])
        w2 = sb("w2", [P, J])
        w2_dg = sb("w2_dg", [P, J, P])
        b2 = sb("b2", [P, 1])
        bin2 = sb("bin2", [P, 1])
        c_t = sb("c_t", [P, KD, B])
        mod_all = sb("mod_all", [P, 4 * KD, B])
        mod = sb("mod", [P, 4 * KD])
        gain = sb("gain", [P, D])
        shift = sb("shift", [P, D])
        wout_g = sb("wout_g", [P, D])

        x_in = sb("x_in", [P, 2, D])
        x_res = sb("x_res", [P, 2, D])
        xn = sb("xn", [P, D])
        h_t = sb("h_t", [P, 2, KD, T])
        xs_t = sb("xs_t", [P, 2, KD, T])
        sz_t = sb("sz_t", [P, 2, KD, T])
        ez = ev = sb("ez", [P, KD, T])
        v_t = u_t = sb("v_t", [P, KD, T])
        dt_t = sb("dt_t", [P, 2, KD, T])
        u_hi = sb("u_hi", [P, D], f32r)
        u_lo = sb("u_lo", [P, D], f32r)
        u_st = sb("u_st", [P, G, D], f32r)
        cb_t = sb("cb_t", [2 * N, T])
        c_st = sb("c_st", [2 * 32, T], f32r)
        b_st = sb("b_st", [P, G, N], f32r)
        b_dg = sb("b_dg", [P, 2, G, N, 32], f32r)
        c_bc = sb("c_bc", [P, 2, N, T])
        decay = sb("decay", [P, KD, SU, N, U])
        dec0 = sb("dec0", [P, 2, SU, N])
        carry = sb("carry", [P, N])
        hs = sb("hs", [P, 4, N, U])
        state = sb("state", [P, KD, N])
        pr = sb("pr", [P, 2, N, T])
        yx = sb("yx", [P, T])
        xn2 = sb("xn2", [P, D])
        h2_t = sb("h2_t", [P, KD, T])
        rel = sb("rel", [P, J, T])
        t1 = rel[:, 0:D // T, :].rearrange("p a b -> p (a b)")
        gm = sb("gm", [P, T])
        c_tmp = gm[:, 0:KD * B].rearrange("p (k b) -> p k b", k=KD)
        norm = sb("norm", [P, 3, 10])
        st, mv, lv, rstd = ([norm[:, n, a:z] for n in range(3)] for a, z in ((0, 6), (6, 8), (8, 9), (9, 10)))
        eps = sb("eps", [P, 1])
        idle = sb("idle", [P, 1])

        work = decay[:, :, :, :, :].rearrange("p a b c d -> p (a b c d)")
        wm4 = work[:, 0:KD * 4 * D].rearrange("p (k n) -> p k n", k=KD)
        wmg = work[:, 0:KD * 2 * D].rearrange("p (k n) -> p k n", k=KD)
        row = lambda n: work[:, (2 * KD + n) * D:(2 * KD + n + 1) * D]
        gamma_b, beta_b, wout_b, bout_b, sign, gate_a, gate_b = (row(n) for n in range(7))
        c_rep = row(7).rearrange("p (k n) -> p k n", k=KD)
        b_out = x_res[0:1, 0, :]
        bout_g = sign[64:65]

        b_ps = pb("b_ps", [P, 2, N * U])
        dn = [pb(f"dense{n}", [P, 512]) for n in range(3)]
        pre_ps = dn[2]
        c_bank = [dn[n] for n in (0, 0, 1, 0)]
        small = pb("small", [P, T])
        y_ps = s_ps = small[:, :]
        cb_ps = small[0:2 * N, :]
        bst_ps = small[:, 0:G * N]

        Q = 16
        N_WEIGHTS = 4 + 5 * 2 + 6
        once = """w_loaded b2_loaded wm_loaded wmg_loaded rows_loaded const_zeroed const_masks sel_copied
        neg_done scal_done c_exp c_one c_rcp silu_c mods_ps mods_done c_rep_done gates_ps sign_done gate_done
        bhi_split batch_ready""".split()
        per_block = {
            "SP": dict(ust_loaded_0=2 * G * Q, ust_loaded_1=2 * G * Q),
            "Pool": dict(u_done=1, xres_done=1, prod_done=UNITS, tg_done=1, x1_done=1),
            "PE": dict(xt_ps=1, xs_ps=1, v_ps=1, u_ps=1, z_ps=1, cb_made=1, bst_made=1, cbc_ps=4,
                       b_ps_done=UNITS, y_ps_done=KD, ust_free=1, res_ps=1, pre_made=1, x2t_ps=1, s_made=1,
                       g_made=1, out_ps=1),
            "ACT": dict(lv0_done=1, lv1_done=1, lv2_done=1, rstd0_done=1, rstd1_done=1, rstd2_done=1,
                        h_done=KD, ab_done=1, ev_done=1, lnv_done=1, uhi_done=1, az_done=1, ez_done=1, lz_done=1,
                        sig_done=1, cb_done=1, cbc_done=4, dec_done=2 * KD, h2_done=KD, rel_done=J),
            "DVE": dict(st0_done=1, st1_done=1, st2_done=1, mv0_done=1, mv1_done=1, mv2_done=1, xn_done=1,
                        xs_done=1, v_done=1, dt_done=1, ulo_done=1, z_done=1, mz_done=1, sz_done=1, chi_done=1,
                        clo_done=1, brep_done=1, bhi_done=1, blo_done=2, bdg_done=1, dec0_done=KD,
                        dec_zeroed=KD, carry_done=UNITS, b_fixed=UNITS, scan_done=UNITS, state_saved=KD,
                        pair_done=KD, yx_done=KD, yz_done=KD, t1_done=1, xn2_done=1, gm_done=1, out_done=1),
        }
        S = {n: sem(n) for n in once + [n for names in per_block.values() for n in names]}
        x_loaded = [sem("x_loaded_even"), sem("x_loaded_odd")]
        stored = [sem("stored_even"), sem("stored_odd")]

        FIRST = 4

        def count_up(eng, name):
            for n, v in per_block[name].items():
                eng.sem_inc(S[n], FIRST * v)

        def x_count(k, p):
            return k * (Q // 2) + (Q - p * (Q // 2))

        def batches(eng, start, part, after_scans=None):
            with eng.Fori(0, B) as batch:
                start(batch)
                k = batch * NB + FIRST
                for m, on in ((-2, "e"), (-1, "ef"), (0, "efs"), (1, "efsb")):
                    part(k + m, m % 2, on)
                with eng.Fori(0, (NB - 4) // 2) as pair:
                    for m in (2, 3):
                        part(k + pair * 2 + m, m % 2, "efsbc")
                for m, on in ((-2, "fsbc"), (-1, "sbc"), (0, "bc"), (1, "c")):
                    part(k + (NB + m), m % 2, on)
                    if after_scans and m == -1:
                        after_scans(k + NB)

        blk = ctx.enter_context(nc.Block(no_gpsimd_drain=True))

        @blk.sync
        def _(sp):
            count_up(sp, "SP")
            for n in range(2):
                sp.sem_inc(x_loaded[n], FIRST * Q // 2)
                sp.sem_inc(stored[n], FIRST * Q // 2)

            def load(dst, src):
                sp.dma_start(dst, src).then_inc(S["w_loaded"], Q)

            sp.dma_start(c_t[:, :, :], ap["c_t"]).then_inc(S["c_exp"], Q)
            load(w_in[:, :, :], ap["w_in_t"].rearrange("(k p) n -> p k n", p=P))
            load(w_dt[:, :, :], ap["w_dt_t"].rearrange("(k p) n -> p k n", p=P))
            load(w_out[:, :, :], ap["w_out_t"].rearrange("(k p) n -> p k n", p=P))
            load(w_cb[:, :, :], ap["w_cb_t"].rearrange("(k p) n -> p k n", p=P))
            for h in range(2):
                load(win2[:, :, h * M:(h + 1) * M], ap["Win"].rearrange("(k p) n -> p k n", p=P))
                load(bin2[h * M:(h + 1) * M, :], ap["bin"].rearrange("(p a) -> p a", a=1))
                for dst, src in ((w1, "W1"), (b1, "b1"), (w2, "W2")):
                    load(dst[h * M:(h + 1) * M, :], ap[src][:, h * J:(h + 1) * J])
            load(b_out, ap["b_out"].rearrange("(a n) -> a n", a=1))
            load(b_in[:, :], ap["b_in_c"])
            load(b_dt[:, :], ap["b_dt_c"])
            load(d_skip[:, :], ap["D_c"])
            load(b_cb[:, :], ap["b_cb"].rearrange("(p a) -> p a", a=1))
            load(neg_a[:, :, :], ap["A_log_c"])
            sp.wait_ge(S["const_zeroed"], 7)
            sp.dma_start(b2[0:M, :], ap["b2"].rearrange("(p a) -> p a", a=1)).then_inc(S["b2_loaded"], Q)
            sp.wait_ge(S["sel_copied"], 1)
            for n, v in enumerate((0, 1, 3, 4)):
                sp.dma_start(wm4[:, :, n * D:(n + 1) * D],
                             ap["wmod"][:, v * D:(v + 1) * D].rearrange("(k p) n -> p k n", p=P)
                             ).then_inc(S["wm_loaded"], Q)
            sp.wait_ge(S["mods_ps"], 1)

            def load_x(k, p):
                sp.dma_start(x_in[:, p, :], ap["x"][bass.ds((k - FIRST) * T, T), :]).then_inc(x_loaded[p], Q)

            def load_gates():
                for n, v in enumerate((2, 5)):
                    sp.dma_start(wmg[:, :, n * D:(n + 1) * D],
                                 ap["wmod"][:, v * D:(v + 1) * D].rearrange("(k p) n -> p k n", p=P)
                                 ).then_inc(S["wmg_loaded"], Q)
                for dst, src in ((gamma_b, "gamma"), (beta_b, "beta"), (bout_b, "bout")):
                    sp.dma_start(dst, ap[src].rearrange("(a n) -> a n", a=1).to_broadcast([P, D])
                                 ).then_inc(S["rows_loaded"], Q)
                for h in range(2):
                    sp.dma_start(wout_b[h * M:(h + 1) * M, :], ap["Wout"]).then_inc(S["rows_loaded"], Q)

            def start(batch):
                k = batch * NB + FIRST
                load_x(k, 0)
                load_x(k + 1, 1)

            def part(s, p, on):
                f, c, e = s + 1, s - 2, s + 2
                if "c" in on:
                    sp.wait_ge(S["out_done"], c + 1)
                    sp.dma_start(ap["out"][bass.ds((c - FIRST) * T, T), :], x_res[:, p, :]).then_inc(stored[p], Q)
                if "s" in on and "e" in on:
                    sp.wait_ge(S["xres_done"], s + 1)
                    load_x(e, p)
                if "f" in on:
                    sp.wait_ge(S["ust_free"], f + 1)
                    for half in range(SU):
                        for quad, (src, done) in enumerate(((u_hi, "uhi_done"), (u_hi, "uhi_done"),
                                                            (u_lo, "ulo_done"), (u_lo, "ulo_done"))):
                            if half == 0:
                                sp.wait_ge(S[done], f + 1)
                            for g in range(half * G // SU, (half + 1) * G // SU):
                                sp.dma_start(u_st[32 * quad:32 * quad + 32, g, :].bitcast(f32),
                                             src[32 * g:32 * g + 32, :].bitcast(f32)
                                             ).then_inc(S[f"ust_loaded_{half}"], Q)

            def after_scans(k):
                sp.wait_ge(S["scan_done"], k * UNITS)
                load_gates()

            load_gates()
            batches(sp, start, part, after_scans)
            sp.wait_ge(S["wmg_loaded"], (B + 1) * (2 * Q))
            sp.wait_ge(S["rows_loaded"], (B + 1) * (5 * Q))
            for n in range(2):
                sp.wait_ge(stored[n], (B * NB + FIRST) * Q // 2)

        @blk.gpsimd
        def _(gp):
            count_up(gp, "Pool")
            f_sel = work[0:64, 0:N * P].rearrange("p (n c) -> p n c", n=N)
            for t, v in ((ident, 0.0), (mask, 0.0), (sel_b, 0.0), (ones, 1.0), (bias_rows, 0.0), (b2, 0.0)):
                gp.memset(t[:, :].bitcast(f32), v).then_inc(S["const_zeroed"], 1)
            gp.memset(f_sel, 0.0).then_inc(S["const_zeroed"], 1)
            gp.wait_ge(S["const_zeroed"], 7)

            def select(view, base, pattern, n):
                gp.affine_select(out=view, in_=view, compare_op=ALU.not_equal, fill=1.0, base=base,
                                 pattern=pattern, channel_multiplier=1).then_inc(S["const_masks"], 1)
                gp.wait_ge(S["const_masks"], n)

            select(ident[:, :], 0, [[-1, P]], 1)
            for q in range(4):
                select(mask[:, :], -32 * q, [[-1, 32]], 2 + q)
            select(sel_b[:, :], -N, [[-1, N]], 6)
            for q in range(2):
                select(f_sel, -32 * q, [[-1, N], [0, P]], 7 + q)

            def start(batch):
                gp.wait_ge(S["batch_ready"], batch + 1)

            def part(s, p, on):
                f, b, q = s + 1, s - 1, 1 - p
                for u in range(UNITS):
                    j, half = u // SU, u % SU
                    if u == 5 and "f" in on:
                        gp.wait_ge(S["dt_done"], f + 1)
                        gp.wait_ge(S["u_ps"], f)
                        gp.tensor_tensor(u_t[:, :, :], dt_t[:, q, :, :], xs_t[:, q, :, :], ALU.mult
                                         ).then_inc(S["u_done"], 1)
                    if u == 5 and "b" in on:
                        gp.wait_ge(S["t1_done"], b + 1)
                        gp.tensor_tensor(t1, t1, gain[:, :], ALU.mult).then_inc(S["tg_done"], 1)
                        gp.wait_ge(S["tg_done"], b + 1)
                        gp.tensor_tensor(x_res[:, q, :], x_res[:, q, :], t1, ALU.add
                                         ).then_inc(S["x1_done"], 1)
                    if "s" in on:
                        gp.wait_ge(S["scan_done"], s * UNITS + (u + 1))
                        if u == 0:
                            gp.wait_ge(S["cbc_done"], s * 4 + 4)
                        if half == 0:
                            gp.wait_ge(S["y_ps_done"], s * KD + (j - 1))
                        gp.tensor_tensor(pr[:, j % 2, :, half * U:(half + 1) * U], hs[:, u % 4, :, :],
                                         c_bc[:, p, :, half * U:(half + 1) * U], ALU.mult
                                         ).then_inc(S["prod_done"], 1)
                    if u == 3 and "s" in on:
                        gp.wait_ge(x_loaded[p], x_count(s, p))
                        gp.wait_ge(stored[p], x_count(s - 2, p))
                        gp.tensor_tensor(x_res[:, p, :], x_in[:, p, :], shift[:, :], ALU.add
                                         ).then_inc(S["xres_done"], 1)

            batches(gp, start, part)

        @blk.tensor
        def _(pe):
            count_up(pe, "PE")
            mm = nc.tensor.matmul
            pe.wait_ge(S["w_loaded"], Q * N_WEIGHTS)
            pe.wait_ge(S["const_masks"], 8)
            pe.wait_ge(S["silu_c"], 1)
            pe.wait_ge(S["wm_loaded"], Q * 4)
            for m in range(4 * KD):
                for j in range(KD):
                    last = mm(dn[0][:, m * B:(m + 1) * B], wm4[:, j, m * P:(m + 1) * P], c_t[:, j, :],
                              start=(j == 0), stop=(j == KD - 1))
            last.then_inc(S["mods_ps"], 1)
            pe.wait_ge(S["mods_done"], 2)

            def start(batch):
                pe.wait_ge(S["c_rep_done"], batch + 1)
                pe.wait_ge(S["wmg_loaded"], batch * (2 * Q) + 2 * Q)
                pe.wait_ge(S["out_done"], batch * NB + FIRST)
                for n in range(2):
                    for j in range(KD):
                        last = mm(dn[n][:, :], c_rep[:, j, :], wmg[:, j, n * D:(n + 1) * D],
                                  start=(j == 0), stop=(j == KD - 1))
                last.then_inc(S["gates_ps"], 1)
                pe.wait_ge(S["batch_ready"], batch + 1)

            def scan_input(s, p, u):
                j, half = u // SU, u % SU
                if u == 0:
                    pe.wait_ge(S["bdg_done"], s + 1)
                if u < SU:
                    pe.wait_ge(S[f"ust_loaded_{half}"], s * (2 * G * Q) + 2 * G * Q)
                pe.wait_ge(S["scan_done"], s * UNITS + (u - 1))
                for g in range(2):
                    for h in range(2):
                        bank = b_ps[:, u % 2, h * 512:(h + 1) * 512].rearrange("p (n t) -> p n t", t=U)
                        last = mm(bank[:, :, g * 32:(g + 1) * 32],
                                  u_st[:, 2 * half + g, j * P:(j + 1) * P],
                                  b_dg[:, p, 2 * half + g, h * HN:(h + 1) * HN, :], start=True, stop=True)
                last.then_inc(S["b_ps_done"], 1)

            def sum_states(s, j):
                pe.wait_ge(S["pair_done"], s * KD + (j + 1))
                pe.wait_ge(S["yx_done"], s * KD + j)
                for n in range(HN):
                    last = mm(y_ps, ident[:, :], pr[:, j % 2, n, :], start=(n == 0),
                              stop=(n == HN - 1))
                last.then_inc(S["y_ps_done"], 1)

            def broadcast_c(f, part4):
                pe.wait_ge(S["clo_done"], f + 1)
                for n in range(4):
                    if part4 == 1 and n == 1:
                        last.then_inc(S["ust_free"], 1)
                    last = mm(c_bank[part4][:, n * T:(n + 1) * T], sel_c[:, 4 * part4 + n, :], c_st[:, :],
                              start=True, stop=True)
                last.then_inc(S["cbc_ps"], 1)

            def transpose4(dst, src, ready):
                for j in range(KD):
                    last = nc.tensor.transpose(dst[:, j * P:(j + 1) * P], src[:, j * P:(j + 1) * P], ident[:, :])
                last.then_inc(ready, 1)

            def project(dst, w, col, src, ready):
                for m in range(KD):
                    for j in range(KD):
                        last = mm(dst[:, m * T:(m + 1) * T], w[:, j, col + m * P:col + (m + 1) * P], src[:, j, :],
                                  start=(j == 0), stop=(j == KD - 1))
                last.then_inc(ready, 1)

            def part(s, p, on):
                f, b, c, q = s + 1, s - 1, s - 2, 1 - p
                small_read = lambda name, v: pe.wait_ge(S[name], v)
                for u in range(UNITS):
                    if u == 0:
                        if "s" in on:
                            scan_input(s, p, 0)
                        if "c" in on:
                            if "b" in on:
                                small_read("yx_done", b * KD + 3)
                            pe.wait_ge(S["h2_done"], c * KD + KD)
                            for j in range(KD):
                                last = mm(s_ps, win2[:, j, :], h2_t[:, j, :], start=(j == 0), stop=(j == KD - 1))
                            last.then_inc(S["s_made"], 1)
                        if "f" in on:
                            pe.wait_ge(S["cbc_done"], f * 4)
                            pe.wait_ge(S["xn_done"], f + 1)
                            transpose4(dn[0], xn, S["xt_ps"])
                        if "b" in on:
                            pe.wait_ge(S["h2_done"], b * KD)
                            mm(pre_ps[:, :], ones[0:64, :], bias_rows[0:64, :], start=True, stop=False)
                            for j in range(KD):
                                last = mm(pre_ps[:, j * P:(j + 1) * P], h_t[:, q, j, :], ident[:, :], start=False,
                                          stop=False)
                            last.then_inc(S["res_ps"], 1)
                    if u == 1:
                        if "s" in on:
                            scan_input(s, p, 1)
                        if "c" in on:
                            if "s" in on:
                                pe.wait_ge(S["z_done"], s + 1)
                            pe.wait_ge(S["rel_done"], c * J + J)
                            for j in range(J):
                                last = mm(dn[1][:, 0:T], w2_dg[:, j, :], rel[:, j, :], start=(j == 0),
                                          stop=(j == J - 1))
                            last.then_inc(S["g_made"], 1)
                        if "b" in on:
                            small_read("rel_done", b * J)
                            sum_states(b, KD - 1)
                    if u == 2:
                        if "s" in on:
                            scan_input(s, p, 2)
                            scan_input(s, p, 3)
                        if "f" in on:
                            pe.wait_ge(S["h_done"], f * KD + KD)
                            project(dn[0], w_in, 0, h_t[:, q, :, :], S["xs_ps"])
                        if "c" in on:
                            pe.wait_ge(S["gm_done"], c + 1)
                            mm(dn[1][:, :], ones[64:P, :], bias_rows[64:P, :], start=True, stop=False)
                            mm(dn[1][:, :], gm[:, :], wout_g[:, :], start=False, stop=True
                               ).then_inc(S["out_ps"], 1)
                    if u == 3:
                        if "f" in on:
                            small_read("yx_done", f * KD - KD)
                            pe.wait_ge(S["xs_done"], f + 1)
                            for j in range(KD):
                                last = mm(cb_ps, w_cb[:, j, :], xs_t[:, q, j, :], start=(j == 0),
                                          stop=(j == KD - 1))
                            last.then_inc(S["cb_made"], 1)
                        if "s" in on:
                            scan_input(s, p, 4)
                        if "f" in on:
                            project(dn[0], w_dt, 0, xs_t[:, q, :, :], S["v_ps"])
                        if "s" in on:
                            if "f" in on:
                                small_read("cb_done", f + 1)
                            sum_states(s, 0)
                    if u == 4:
                        if "s" in on:
                            scan_input(s, p, 5)
                        if "b" in on:
                            pe.wait_ge(S["yz_done"], b * KD + KD)
                            for j in range(KD):
                                last = mm(pre_ps[:, :], sz_t[:, q, j, :], w_out[:, j, :], start=False,
                                          stop=(j == KD - 1))
                            last.then_inc(S["pre_made"], 1)
                        if "f" in on:
                            if "s" in on:
                                small_read("yx_done", s * KD + 1)
                            pe.wait_ge(S["brep_done"], f + 1)
                            for g in range(G):
                                last = mm(bst_ps[:, g * N:(g + 1) * N],
                                          b_rep[:, g, :, :].rearrange("p a b -> p (a b)"), sel_b[:, :],
                                          start=True, stop=True)
                            last.then_inc(S["bst_made"], 1)
                    if u == 5:
                        if "s" in on:
                            scan_input(s, p, 6)
                        if "f" in on:
                            pe.wait_ge(S["v_done"], f + 1)
                            broadcast_c(f, 0)
                            if "c" in on:
                                pe.wait_ge(S["out_done"], c + 1)
                            elif "s" in on:
                                pe.wait_ge(S["z_done"], s + 1)
                            pe.wait_ge(S["u_done"], f + 1)
                            transpose4(dn[1], u_t[:, :, :].rearrange("p a b -> p (a b)"), S["u_ps"])
                        if "s" in on:
                            if "f" in on:
                                small_read("blo_done", f * 2 + 2)
                            sum_states(s, 1)
                    if u == 6:
                        if "s" in on:
                            scan_input(s, p, 7)
                        if "f" in on:
                            for part4, bank_read, v in ((1, "cbc_done", f * 4 + 1), (2, "ulo_done", f + 1),
                                                        (3, "cbc_done", f * 4 + 2)):
                                pe.wait_ge(S[bank_read], v)
                                broadcast_c(f, part4)
                            pe.wait_ge(S["cbc_done"], f * 4 + 3)
                            project(dn[1], w_in, D, h_t[:, q, :, :], S["z_ps"])
                    if u == 7:
                        if "b" in on:
                            pe.wait_ge(S["t1_done"], b + 1)
                            pe.wait_ge(S["xn2_done"], b + 1)
                            transpose4(pre_ps, xn2, S["x2t_ps"])
                        if "s" in on:
                            sum_states(s, 2)

            batches(pe, start, part)

        @blk.scalar
        def _(act):
            count_up(act, "ACT")
            A = nc.scalar.activation
            nc.scalar.preload_act_table_set("natural_log_exp_and_others")
            act.wait_ge(S["c_exp"], Q)
            A(c_tmp[:, :, :], c_t[:, :, :], ACT.Exp, scale=-1.0).then_inc(S["c_exp"], 1)
            act.wait_ge(S["w_loaded"], Q * N_WEIGHTS)
            A(neg_a[:, :, :], neg_a[:, :, :], ACT.Exp).then_inc(S["neg_done"], 1)

            def start(batch):
                act.wait_ge(S["scal_done"], 1)
                act.wait_ge(S["batch_ready"], batch + 1)

            def decays(k, p, j, h):
                if h == 0:
                    if j == 0:
                        act.wait_ge(S["dt_done"], k + 1)
                    act.wait_ge(S["scan_done"], k * UNITS + (SU * (j + 1) - UNITS))
                for n in range(h * HN, (h + 1) * HN):
                    last = A(decay[:, j, :, n, :], dt_t[:, p, j, :].rearrange("p (s t) -> p s t", s=SU), ACT.Exp,
                             scale=neg_a[:, j, n:n + 1])
                last.then_inc(S["dec_done"], 1)

            def inv_std(n, k):
                act.wait_ge(S[f"mv{n}_done"], k + 1)
                A(lv[n][:, :], mv[n][:, 1:2], ACT.Ln, bias=eps[:, :]).then_inc(S[f"lv{n}_done"], 1)
                act.wait_ge(S[f"lv{n}_done"], k + 1)
                A(rstd[n][:, :], lv[n][:, :], ACT.Exp, scale=-0.5).then_inc(S[f"rstd{n}_done"], 1)

            def modulate(dst, psum, done, scale, shift_):
                for j in range(KD):
                    A(dst[:, j, :], psum[:, j * T:(j + 1) * T], ACT.Identity, scale=mod[:, scale + j:scale + j + 1],
                      bias=mod[:, shift_ + j:shift_ + j + 1]).then_inc(done, 1)

            def copy_c(f, q, part4):
                act.wait_ge(S["cbc_ps"], f * 4 + (part4 + 1))
                A(c_bc[:, q, 4 * part4:4 * part4 + 4, :], c_bank[part4][:, :].rearrange("p (n t) -> p n t", n=4),
                  ACT.Copy).then_inc(S["cbc_done"], 1)

            def part(s, p, on):
                f, b, c, e, q = s + 1, s - 1, s - 2, s + 2, 1 - p
                for u in range(UNITS):
                    if u == 0 and "c" in on:
                        act.wait_ge(S["s_made"], c + 1)
                        act.wait_ge(S["g_made"], c)
                        act.wait_ge(S["x1_done"], c + 1)
                        for j in range(J):
                            A(rel[:, j, :], s_ps, ACT.Relu, scale=w1[:, j:j + 1], bias=b1[:, j:j + 1]
                              ).then_inc(S["rel_done"], 1)
                    if u == 0 and "f" in on:
                        act.wait_ge(S["xt_ps"], f + 1)
                        act.wait_ge(S["res_ps"], f - 1)
                        modulate(h_t[:, q, :, :], dn[0], S["h_done"], KD, 0)
                    if "s" in on:
                        for half_tile in {0: (3,), 1: (4,), 2: (5,), 3: (6,), 4: (7,)}.get(u, ()):
                            decays(s, p, half_tile // 2, half_tile % 2)
                    if u == 3 and "f" in on:
                        act.wait_ge(S["cb_made"], f + 1)
                        act.wait_ge(S["brep_done"], f)
                        A(cb_t[:, :], cb_ps, ACT.Identity, bias=b_cb[:, :]).then_inc(S["cb_done"], 1)
                    if u == 2 and "s" in on:
                        act.wait_ge(S["z_done"], s + 1)
                        act.wait_ge(S["dt_done"], s + 1)
                        A(ez[:, :, :], sz_t[:, p, :, :], ACT.Abs).then_inc(S["az_done"], 1)
                        act.wait_ge(S["az_done"], s + 1)
                        A(ez[:, :, :], ez[:, :, :], ACT.Exp, scale=-1.0).then_inc(S["ez_done"], 1)
                        act.wait_ge(S["ez_done"], s + 1)
                        A(ez[:, :, :], ez[:, :, :], ACT.Ln, bias=1.0).then_inc(S["lz_done"], 1)
                    if u == 3 and "s" in on:
                        act.wait_ge(S["mz_done"], s + 1)
                        A(ez[:, :, :], ez[:, :, :], ACT.Exp).then_inc(S["sig_done"], 1)
                    if u == 4 and "f" in on:
                        act.wait_ge(S["v_done"], f + 1)
                        act.wait_ge(S["sz_done"], f)
                        A(ev[:, :, :], v_t[:, :, :], ACT.Abs).then_inc(S["ab_done"], 1)
                        act.wait_ge(S["ab_done"], f + 1)
                        A(ev[:, :, :], ev[:, :, :], ACT.Exp, scale=-1.0).then_inc(S["ev_done"], 1)
                        act.wait_ge(S["ev_done"], f + 1)
                        A(ev[:, :, :], ev[:, :, :], ACT.Ln, bias=1.0).then_inc(S["lnv_done"], 1)
                    if u == 5 and "f" in on:
                        decays(f, q, 0, 0)
                    if u == 5 and "b" in on:
                        inv_std(1, b)
                    if u == 5 and "f" in on:
                        act.wait_ge(S["prod_done"], f * UNITS - UNITS)
                        copy_c(f, q, 0)
                        act.wait_ge(S["ust_loaded_1"], f * (2 * G * Q))
                        act.wait_ge(S["u_ps"], f + 1)
                        A(u_hi[:, :], dn[1][:, :], ACT.Copy).then_inc(S["uhi_done"], 1)
                    if u == 6:
                        if "f" in on:
                            for part4 in (1, 2, 3):
                                copy_c(f, q, part4)
                        if "b" in on:
                            inv_std(2, b)
                        if "e" in on:
                            inv_std(0, e)
                        if "f" in on:
                            decays(f, q, 0, 1)
                    if u == 7 and "b" in on:
                        act.wait_ge(S["x2t_ps"], b + 1)
                        act.wait_ge(S["s_made"], b)
                        modulate(h2_t, pre_ps, S["h2_done"], 3 * KD, 2 * KD)
                    if u == 7 and "f" in on:
                        decays(f, q, 1, 0)

            batches(act, start, part)

        @blk.vector
        def _(dve):
            count_up(dve, "DVE")
            V = nc.vector
            dve.wait_ge(S["const_masks"], 8)
            V.tensor_copy(sel_c[:, :, :], work[0:64, 0:N * P].rearrange("p (n c) -> p n c", n=N)
                          ).then_inc(S["sel_copied"], 1)
            V.memset(eps[:, :], EPS)
            dve.wait_ge(S["c_exp"], Q + 1)
            V.tensor_scalar(c_tmp[:, :, :], c_tmp[:, :, :], 1.0, None, ALU.add).then_inc(S["c_one"], 1)
            dve.wait_ge(S["c_one"], 1)
            V.reciprocal(c_tmp[:, :, :], c_tmp[:, :, :]).then_inc(S["c_rcp"], 1)
            dve.wait_ge(S["c_rcp"], 1)
            V.tensor_tensor(c_t[:, :, :], c_t[:, :, :], c_tmp[:, :, :], ALU.mult).then_inc(S["silu_c"], 1)
            dve.wait_ge(S["neg_done"], 1)
            V.tensor_scalar(neg_a[:, :, :], neg_a[:, :, :], -1.0, None, ALU.mult)
            dve.wait_ge(S["w_loaded"], Q * N_WEIGHTS)
            dve.wait_ge(S["b2_loaded"], Q)
            V.scalar_tensor_tensor(b1[:, :], w1[:, :], bin2[:, :], b1[:, :], ALU.mult, ALU.add
                                   ).then_inc(S["scal_done"], 1)
            for j in range(J):
                V.tensor_scalar(w2_dg[:, j, :], ident[:, :], w2[:, j:j + 1], None, ALU.mult)
            V.tensor_copy(bias_rows[0:1, :], b_out).then_inc(S["bhi_split"], 1)
            dve.wait_ge(S["bhi_split"], 1)
            V.tensor_tensor(bias_rows[32:33, :], b_out, bias_rows[0:1, :].bitcast(f32), ALU.subtract)
            dve.wait_ge(S["mods_ps"], 1)
            for n, plus in enumerate((0.0, 1.0, 0.0, 1.0)):
                last = V.tensor_scalar(mod_all[:, n * KD:(n + 1) * KD, :],
                                       dn[0][:, n * KD * B:(n + 1) * KD * B].rearrange("p (m b) -> p m b", b=B),
                                       plus, None, ALU.add)
            last.then_inc(S["mods_done"], 2)

            def start(batch):
                dve.wait_ge(S["mods_done"], 2)
                dve.wait_ge(S["silu_c"], 1)
                V.tensor_copy(c_rep[:, :, :], c_t[:, :, bass.ds(batch, 1)].to_broadcast([P, KD, P])
                              ).then_inc(S["c_rep_done"], 1)
                V.tensor_copy(mod[:, :], mod_all[:, :, bass.ds(batch, 1)].rearrange("p m b -> p (m b)"))
                V.memset(state[:, :, :], 0.0)
                dve.wait_ge(S["rows_loaded"], batch * (5 * Q) + 5 * Q)
                dve.wait_ge(S["gates_ps"], batch + 1)
                for n, gate in enumerate((gate_a, gate_b)):
                    V.tensor_scalar(sign, dn[n][:, :], 0.0, 2.0, ALU.is_ge, ALU.mult).then_inc(S["sign_done"], 1)
                    dve.wait_ge(S["sign_done"], batch * 6 + (3 * n + 1))
                    V.tensor_scalar(sign, sign, -1.0, None, ALU.add).then_inc(S["sign_done"], 1)
                    dve.wait_ge(S["sign_done"], batch * 6 + (3 * n + 2))
                    V.tensor_tensor(gate, sign, dn[n][:, :], ALU.mult).then_inc(S["sign_done"], 1)
                    dve.wait_ge(S["sign_done"], batch * 6 + (3 * n + 3))
                    V.scalar_tensor_tensor(gate, gate, 0.25, sign, ALU.max, ALU.mult).then_inc(S["gate_done"], 1)
                    dve.wait_ge(S["gate_done"], batch * 2 + (n + 1))
                V.tensor_tensor(gain[:, :], gate_a, gamma_b, ALU.mult)
                V.tensor_tensor(shift[:, :], gate_a, beta_b, ALU.mult)
                V.tensor_tensor(wout_g[:, :], gate_b, wout_b, ALU.mult)
                V.tensor_tensor(bout_g, gate_b[64:65, :], bout_b[64:65, :], ALU.mult
                                ).then_inc(S["bhi_split"], 1)
                dve.wait_ge(S["bhi_split"], batch * 2 + 2)
                V.tensor_copy(bias_rows[64:65, :], bout_g).then_inc(S["bhi_split"], 1)
                dve.wait_ge(S["bhi_split"], batch * 2 + 3)
                V.tensor_tensor(bias_rows[96:97, :], bout_g, bias_rows[64:65, :].bitcast(f32), ALU.subtract
                                ).then_inc(S["batch_ready"], 1)
                dve.wait_ge(S["batch_ready"], batch + 1)

            def set_aside(s, j):
                dve.wait_ge(S["dec_done"], s * (2 * KD) + (2 * j + 2))
                V.tensor_copy(dec0[:, j % 2, :, :], decay[:, j, :, :, 0]).then_inc(S["dec0_done"], 1)

            def zero(s, j):
                dve.wait_ge(S["dec0_done"], s * KD + (j + 1))
                V.memset(decay[:, j, :, :, 0], 0.0).then_inc(S["dec_zeroed"], 1)

            def carry_in(s, u):
                j, half = u // SU, u % SU
                if half == 0:
                    dve.wait_ge(S["dec0_done"], s * KD + (j + 1))
                    dve.wait_ge(S["state_saved"], s * KD + (j + 1 - KD))
                    before = state[:, j, :]
                else:
                    before = hs[:, (u - 1) % 4, :, U - 1]
                    dve.wait_ge(S["scan_done"], s * UNITS + u)
                V.tensor_tensor(carry[:, :], dec0[:, j % 2, half, :], before, ALU.mult).then_inc(S["carry_done"], 1)

            def add_carry(s, u):
                dve.wait_ge(S["carry_done"], s * UNITS + (u + 1))
                dve.wait_ge(S["b_ps_done"], s * UNITS + (u + 1))
                heads = b_ps[:, u % 2, :].rearrange("p (n t) -> p n t", t=U)[:, :, 0]
                V.tensor_tensor(heads, heads, carry[:, :], ALU.add).then_inc(S["b_fixed"], 1)

            def scan(s, u):
                j, half = u // SU, u % SU
                dve.wait_ge(S["b_fixed"], s * UNITS + (u + 1))
                dve.wait_ge(S["dec_zeroed"], s * KD + (j + 1))
                dve.wait_ge(S["prod_done"], s * UNITS + (u - 3))
                V.tensor_tensor_scan(hs[:, u % 4, :, :].rearrange("p n t -> p (n t)"),
                                     decay[:, j, half, :, :].rearrange("p n t -> p (n t)"), b_ps[:, u % 2, :], 0.0,
                                     ALU.mult, ALU.add).then_inc(S["scan_done"], 1)

            def save_state(s, j):
                last = SU * j + SU - 1
                dve.wait_ge(S["scan_done"], s * UNITS + (last + 1))
                V.tensor_copy(state[:, j, :], hs[:, last % 4, :, U - 1]).then_inc(S["state_saved"], 1)

            def add_pairs(s, j):
                dve.wait_ge(S["prod_done"], s * UNITS + SU * (j + 1))
                V.tensor_tensor(pr[:, j % 2, 0:HN, :], pr[:, j % 2, 0:HN, :], pr[:, j % 2, HN:N, :], ALU.add
                                ).then_inc(S["pair_done"], 1)

            def skip_y(s, p, j):
                dve.wait_ge(S["yz_done"], s * KD + j)
                dve.wait_ge(S["y_ps_done"], s * KD + (j + 1))
                V.scalar_tensor_tensor(yx[:, :], xs_t[:, p, j, :], d_skip[:, j:j + 1], y_ps,
                                       ALU.mult, ALU.add).then_inc(S["yx_done"], 1)

            def gate_y(s, p, j):
                dve.wait_ge(S["yx_done"], s * KD + (j + 1))
                V.tensor_tensor(sz_t[:, p, j, :], sz_t[:, p, j, :], yx[:, :], ALU.mult).then_inc(S["yz_done"], 1)

            def moments(n, k, src):
                V.bn_stats(st[n][:, :], src).then_inc(S[f"st{n}_done"], 1)
                dve.wait_ge(S[f"st{n}_done"], k + 1)
                V.memset(idle[:, :], 0.0)
                V.bn_aggr(mv[n][:, :], st[n][:, :]).then_inc(S[f"mv{n}_done"], 1)

            def normalize(n, k, dst, src, done):
                dve.wait_ge(S[f"rstd{n}_done"], k + 1)
                V.tensor_scalar(dst, src, mv[n][:, 0:1], rstd[n][:, :], ALU.subtract, ALU.mult).then_inc(done, 1)

            def bias4(dst, psum, bias, done):
                V.tensor_tensor(dst, psum[:, :].rearrange("p (k t) -> p k t", k=KD),
                                bias.unsqueeze(2).to_broadcast([P, KD, T]), ALU.add).then_inc(done, 1)

            def add_bias(f, q):
                dve.wait_ge(S["v_ps"], f + 1)
                dve.wait_ge(S["u_ps"], f)
                bias4(v_t[:, :, :], dn[0], b_dt[:, :], S["v_done"])

            def split_c(f):
                dve.wait_ge(S["cb_done"], f + 1)
                dve.wait_ge(S["cbc_ps"], f * 4)
                V.tensor_copy(c_st[0:32, :], cb_t[:, :]).then_inc(S["chi_done"], 1)
                dve.wait_ge(S["bst_made"], f)
                V.tensor_copy(b_rep[:, :, :, :],
                              cb_t[:, :].rearrange("p (g o t) -> p g o t", g=G, o=1
                                                   ).to_broadcast([2 * N, G, 4, 32])
                              ).then_inc(S["brep_done"], 1)
                dve.wait_ge(S["chi_done"], f + 1)
                V.tensor_tensor(c_st[32:64, :], cb_t[:, :], c_st[0:32, :].bitcast(f32), ALU.subtract
                                ).then_inc(S["clo_done"], 1)

            def softplus(f, q):
                dve.wait_ge(S["lnv_done"], f + 1)
                V.scalar_tensor_tensor(dt_t[:, q, :, :].rearrange("p k t -> p (k t)"),
                                       v_t[:, :, :].rearrange("p k t -> p (k t)"), 0.0,
                                       ev[:, :, :].rearrange("p k t -> p (k t)"), ALU.max, ALU.add
                                       ).then_inc(S["dt_done"], 1)

            def split_b(f):
                dve.wait_ge(S["bst_made"], f + 1)
                dve.wait_ge(S["bdg_done"], f)
                src = bst_ps.rearrange("p (g n) -> p g n", g=G)
                V.tensor_copy(b_st[:, :, :], src).then_inc(S["bhi_done"], 1)
                dve.wait_ge(S["bhi_done"], f + 1)
                for quad in (1, 3):
                    rows = slice(32 * quad, 32 * quad + 32)
                    V.tensor_tensor(b_st[rows, :, :], src[rows], b_st[rows, :, :].bitcast(f32),
                                    ALU.subtract).then_inc(S["blo_done"], 1)

            def spread_b(f, q):
                dve.wait_ge(S["blo_done"], f * 2 + 2)
                for g in range(G):
                    last = V.tensor_tensor(
                        b_dg[:, q, g, :, :], mask[:, :].unsqueeze(1).to_broadcast([P, N, 32]),
                        b_st[:, g, :].bitcast(f32).unsqueeze(2).to_broadcast([P, N, 32]), ALU.mult)
                last.then_inc(S["bdg_done"], 1)

            def part(s, p, on):
                f, b, c, e, q = s + 1, s - 1, s - 2, s + 2, 1 - p
                if "s" in on:
                    dve.wait_ge(S["z_ps"], s + 1)
                    bias4(sz_t[:, p, :, :], dn[1], b_in[:, KD:2 * KD], S["z_done"])
                    set_aside(s, 0)
                    carry_in(s, 0)
                    zero(s, 0)
                    add_carry(s, 0)
                    scan(s, 0)
                if "b" in on:
                    add_pairs(b, KD - 1)
                if "s" in on:
                    carry_in(s, 1)
                    add_carry(s, 1)
                    scan(s, 1)
                if "c" in on:
                    dve.wait_ge(S["g_made"], c + 1)
                    dve.wait_ge(S["out_ps"], c)
                    V.tensor_scalar(gm[:, :], dn[1][:, 0:T], b2[:, :], None, ALU.add).then_inc(S["gm_done"], 1)
                if "s" in on:
                    set_aside(s, 1)
                if "b" in on:
                    skip_y(b, q, 3)
                if "s" in on:
                    carry_in(s, 2)
                    zero(s, 1)
                    save_state(s, 0)
                    add_carry(s, 2)
                    scan(s, 2)
                if "b" in on:
                    gate_y(b, q, 3)
                if "s" in on:
                    carry_in(s, 3)
                    add_carry(s, 3)
                    scan(s, 3)
                if "f" in on:
                    dve.wait_ge(S["xs_ps"], f + 1)
                    bias4(xs_t[:, q, :, :], dn[0], b_in[:, 0:KD], S["xs_done"])
                if "s" in on:
                    set_aside(s, 2)
                    add_pairs(s, 0)
                    zero(s, 2)
                if "c" in on:
                    dve.wait_ge(S["out_ps"], c + 1)
                    V.tensor_tensor(x_res[:, p, :], x_res[:, p, :], dn[1][:, :], ALU.add
                                    ).then_inc(S["out_done"], 1)
                if "s" in on:
                    dve.wait_ge(S["lz_done"], s + 1)
                    flat = lambda t: t.rearrange("p k t -> p (k t)")
                    V.scalar_tensor_tensor(flat(ez[:, :, :]), flat(sz_t[:, p, :, :]), 0.0, flat(ez[:, :, :]), ALU.min,
                                           ALU.subtract).then_inc(S["mz_done"], 1)
                    carry_in(s, 4)
                    save_state(s, 1)
                    add_carry(s, 4)
                    scan(s, 4)
                    add_pairs(s, 1)
                    dve.wait_ge(S["sig_done"], s + 1)
                    V.tensor_tensor(sz_t[:, p, :, :], sz_t[:, p, :, :], ez[:, :, :], ALU.mult
                                    ).then_inc(S["sz_done"], 1)
                if "f" in on:
                    dve.wait_ge(S["v_ps"], f + 1)
                    dve.wait_ge(S["u_ps"], f)
                    bias4(v_t[:, :, :], dn[0], b_dt[:, :], S["v_done"])
                    split_c(f)
                if "s" in on:
                    skip_y(s, p, 0)
                    dve.wait_ge(S["sz_done"], s + 1)
                    gate_y(s, p, 0)
                if "f" in on:
                    softplus(f, q)
                if "b" in on:
                    dve.wait_ge(S["pre_made"], b + 1)
                    moments(1, b, pre_ps[:, :])
                if "f" in on:
                    split_b(f)
                if "s" in on:
                    carry_in(s, 5)
                    set_aside(s, 3)
                    add_carry(s, 5)
                    zero(s, 3)
                if "b" in on:
                    dve.wait_ge(S["g_made"], b)
                    normalize(1, b, t1, pre_ps[:, :], S["t1_done"])
                if "s" in on:
                    scan(s, 5)
                if "f" in on:
                    dve.wait_ge(S["uhi_done"], f + 1)
                    V.tensor_tensor(u_lo[:, :], dn[1][:, :], u_hi[:, :].bitcast(f32), ALU.subtract
                                    ).then_inc(S["ulo_done"], 1)
                if "s" in on:
                    carry_in(s, 6)
                    skip_y(s, p, 1)
                    save_state(s, 2)
                    add_carry(s, 6)
                    gate_y(s, p, 1)
                    scan(s, 6)
                if "b" in on:
                    dve.wait_ge(S["x1_done"], b + 1)
                    moments(2, b, x_res[:, q, :])
                if "e" in on:
                    dve.wait_ge(x_loaded[p], x_count(e, p))
                    moments(0, e, x_in[:, p, :])
                if "b" in on:
                    dve.wait_ge(S["x2t_ps"], b)
                    normalize(2, b, xn2[:, :], x_res[:, q, :], S["xn2_done"])
                if "s" in on:
                    add_pairs(s, 2)
                if "s" in on:
                    carry_in(s, 7)
                    add_carry(s, 7)
                if "e" in on:
                    dve.wait_ge(S["xt_ps"], e)
                    normalize(0, e, xn[:, :], x_in[:, p, :], S["xn_done"])
                if "f" in on:
                    spread_b(f, q)
                if "s" in on:
                    skip_y(s, p, 2)
                    scan(s, 7)
                    gate_y(s, p, 2)
                    save_state(s, 3)

            batches(dve, start, part)


def kernel(L0_attn_x, L0_attn_w_in, L0_attn_b_in, L0_attn_w_dt, L0_attn_b_dt, L0_attn_A_log, L0_attn_w_B,
           L0_attn_b_B, L0_attn_w_C, L0_attn_b_C, L0_attn_D, L0_attn_w_out, L0_attn_b_out, L0_attn_gamma,
           L0_attn_beta, L0_ffn_Win, L0_ffn_bin_, L0_ffn_W1, L0_ffn_b1, L0_ffn_W2, L0_ffn_b2, L0_ffn_Wout,
           L0_ffn_bout, L0_c, L0_wmod):
    import numpy as np
    import concourse.bacc as bacc
    from concourse import mybir
    from concourse.bass_utils import run_bass_kernel_spmd

    B, L, D = L0_attn_x.shape
    N = L0_attn_A_log.shape[1]
    M, INNER = L0_ffn_W1.shape
    P = 128
    a = np.asarray
    columns = lambda v: a(v).reshape(-1, P).T
    arrays = {
        "x": a(L0_attn_x).reshape(B * L, D),
        "w_in_t": a(L0_attn_w_in).T, "w_dt_t": a(L0_attn_w_dt).T, "w_out_t": a(L0_attn_w_out).T,
        "w_cb_t": np.concatenate([a(L0_attn_w_C), a(L0_attn_w_B)]).T,
        "b_cb": np.concatenate([a(L0_attn_b_C), a(L0_attn_b_B)]),
        "b_in_c": columns(L0_attn_b_in), "b_dt_c": columns(L0_attn_b_dt), "D_c": columns(L0_attn_D),
        "A_log_c": a(L0_attn_A_log).reshape(-1, P, N).transpose(1, 0, 2),
        "b_out": L0_attn_b_out, "gamma": L0_attn_gamma, "beta": L0_attn_beta,
        "Win": L0_ffn_Win, "bin": L0_ffn_bin_, "W1": L0_ffn_W1, "b1": L0_ffn_b1, "W2": L0_ffn_W2,
        "b2": L0_ffn_b2, "Wout": L0_ffn_Wout, "bout": L0_ffn_bout,
        "c_t": a(L0_c).T.reshape(-1, P, B).transpose(1, 0, 2), "wmod": L0_wmod,
    }
    arrays = {n: np.ascontiguousarray(v) for n, v in arrays.items()}
    nc = bacc.Bacc("TRN2", target_bir_lowering=False, num_devices=1)
    ap = {n: nc.dram_tensor(f"in_{n}", v.shape, mybir.dt.from_np(v.dtype), kind="ExternalInput").ap()
          for n, v in arrays.items()}
    ap["out"] = nc.dram_tensor("out_dram", (B * L, D), mybir.dt.float32, kind="ExternalOutput").ap()
    build_program(nc, ap, B, L, D, N, M, INNER)
    r = run_bass_kernel_spmd(nc, [{f"in_{n}": v for n, v in arrays.items()}], core_ids=[0])
    return r.results[0]["out_dram"].reshape(B, L, D)
```
